# Optimizing a Trainium2 kernel written in Bass

```python
import numpy as np
import jax
import jax.numpy as jnp

def _softmax(x, axis=-1):
    return jax.nn.softmax(x, axis=axis)
def _gelu(x):
    return jax.nn.gelu(x, approximate=True)
def _silu(x):
    return jax.nn.silu(x)
def _sigmoid(x):
    return jax.nn.sigmoid(x)
def _layernorm(x, axis=-1, eps=1e-5):
    m = jnp.mean(x, axis=axis, keepdims=True)
    v = jnp.var(x, axis=axis, keepdims=True)
    return (x - m) / jnp.sqrt(v + eps)
def _scatter_add(tgt, idx, src, axis=0):
    return tgt.at[idx].add(src)
def _segment_sum(src, seg, n):
    return jax.ops.segment_sum(src, seg, n)

kernel_name = 'mk_conv_preact_d1_conv_nhwc384_839e98'

def setup_inputs(seed: int = 0):
    np.random.seed(seed)
    _w = jnp.asarray
    def _rec_inputs():
        import jax
        import jax.numpy as jnp
        _gk = jax.random.key(seed)
        x = -0.000357 + 1 * jax.random.normal(jax.random.fold_in(_gk, 1), (16, 56, 56, 384), jnp.float32)
        return x
    x = _rec_inputs()
    def _L0_conv_setup():
        import jax, jax.numpy as jnp
        import numpy as np
        WS = 7
        HEADS = 12
        HEAD_DIM = 32
        EMBED = 384
        SHIFTED = True
        DISP = WS // 2
        N = WS * WS
        NEG = float('-inf')

        def _shift_masks():
            ul = np.zeros((N, N), np.float32)
            ul[-DISP * WS:, :-DISP * WS] = NEG
            ul[:-DISP * WS, -DISP * WS:] = NEG
            lr = np.zeros((WS, WS, WS, WS), np.float32)
            lr[:, -DISP:, :, :-DISP] = NEG
            lr[:, :-DISP, :, -DISP:] = NEG
            lr = lr.reshape(N, N)
            return (ul, lr)

        def _rel_indices():
            idx = np.array([[x, y] for x in range(WS) for y in range(WS)])
            rel = idx[None, :, :] - idx[:, None, :] + WS - 1
            return rel
        key = jax.random.key(seed)
        k1, k2, k3, k4, k5 = jax.random.split(key, 5)
        B, H, W = (16, 56, 56)
        x = jax.random.normal(k1, (B, H, W, EMBED), jnp.float32)
        w_qkv = jax.random.normal(k2, (3 * HEADS * HEAD_DIM, EMBED), jnp.float32) * 0.02
        pos_emb = jax.random.normal(k3, (2 * WS - 1, 2 * WS - 1), jnp.float32)
        w_out = jax.random.normal(k4, (EMBED, HEADS * HEAD_DIM), jnp.float32) * 0.02
        b_out = jax.random.normal(k5, (EMBED,), jnp.float32) * 0.02
        return {'x': x, 'w_qkv': w_qkv, 'pos_emb': pos_emb, 'w_out': w_out, 'b_out': b_out}
    _L0_conv_all = _L0_conv_setup()
    _L0_conv_in = {k: v for k, v in _L0_conv_all.items() if k in ('w_qkv', 'pos_emb', 'w_out', 'b_out', )}
    del _L0_conv_all

    return {
        "x": x,
        "L0_conv_w_qkv": _L0_conv_in["w_qkv"],
        "L0_conv_pos_emb": _L0_conv_in["pos_emb"],
        "L0_conv_w_out": _L0_conv_in["w_out"],
        "L0_conv_b_out": _L0_conv_in["b_out"],
    }

def reference(x, L0_conv_w_qkv, L0_conv_pos_emb, L0_conv_w_out, L0_conv_b_out):
    import jax
    import jax.numpy as jnp
    def _L0_conv_ref(x, w_qkv, pos_emb, w_out, b_out):
        import jax, jax.numpy as jnp
        import numpy as np
        WS = 7
        HEADS = 12
        HEAD_DIM = 32
        EMBED = 384
        SHIFTED = True
        DISP = WS // 2
        N = WS * WS
        NEG = float('-inf')

        def _shift_masks():
            ul = np.zeros((N, N), np.float32)
            ul[-DISP * WS:, :-DISP * WS] = NEG
            ul[:-DISP * WS, -DISP * WS:] = NEG
            lr = np.zeros((WS, WS, WS, WS), np.float32)
            lr[:, -DISP:, :, :-DISP] = NEG
            lr[:, :-DISP, :, -DISP:] = NEG
            lr = lr.reshape(N, N)
            return (ul, lr)

        def _rel_indices():
            idx = np.array([[x, y] for x in range(WS) for y in range(WS)])
            rel = idx[None, :, :] - idx[:, None, :] + WS - 1
            return rel
        B, H, W, _ = x.shape
        nwh, nww = (H // WS, W // WS)
        nw = nwh * nww
        scale = HEAD_DIM ** (-0.5)
        if SHIFTED:
            x = jnp.roll(x, shift=(-DISP, -DISP), axis=(1, 2))
        qkv = x @ w_qkv.T
        q, k, v = jnp.split(qkv, 3, axis=-1)

        def win(t):
            t = t.reshape(B, nwh, WS, nww, WS, HEADS, HEAD_DIM)
            t = t.transpose(0, 5, 1, 3, 2, 4, 6)
            return t.reshape(B, HEADS, nw, N, HEAD_DIM)
        q, k, v = (win(q), win(k), win(v))
        dots = jnp.einsum('bhwid,bhwjd->bhwij', q, k) * scale
        rel = _rel_indices()
        dots = dots + pos_emb[rel[:, :, 0], rel[:, :, 1]]
        if SHIFTED:
            ul, lr = _shift_masks()
            mask = np.zeros((nw, N, N), np.float32)
            mask[-nww:] += ul
            mask[nww - 1::nww] += lr
            dots = dots + jnp.asarray(mask)
        attn = jax.nn.softmax(dots, axis=-1)
        out = jnp.einsum('bhwij,bhwjd->bhwid', attn, v)
        out = out.reshape(B, HEADS, nwh, nww, WS, WS, HEAD_DIM)
        out = out.transpose(0, 2, 4, 3, 5, 1, 6).reshape(B, H, W, HEADS * HEAD_DIM)
        out = out @ w_out.T + b_out
        if SHIFTED:
            out = jnp.roll(out, shift=(DISP, DISP), axis=(1, 2))
        return out

    def _gn(v, G=32, eps=1e-5):
        B_, H_, W_, C_ = v.shape
        g = v.reshape(B_, H_, W_, G, C_ // G)
        m = jnp.mean(g, axis=(1, 2, 4), keepdims=True)
        s = jnp.var(g, axis=(1, 2, 4), keepdims=True)
        return ((g - m) / jnp.sqrt(s + eps)).reshape(v.shape)

    def _ln_c(v, eps=1e-6):
        m = jnp.mean(v, axis=-1, keepdims=True)
        s = jnp.var(v, axis=-1, keepdims=True)
        return (v - m) / jnp.sqrt(s + eps)

    def _ln_t(v, eps=1e-5):
        m = jnp.mean(v, axis=-1, keepdims=True)
        s = jnp.var(v, axis=-1, keepdims=True)
        return (v - m) / jnp.sqrt(s + eps)

    def _to_tokens(v):
        B_, H_, W_, C_ = v.shape
        return v.reshape(B_, H_ * W_, C_)
    def _from_tokens(t, like):
        return t.reshape(like.shape)

    x = x + _L0_conv_ref(_gn(x), L0_conv_w_qkv, L0_conv_pos_emb, L0_conv_w_out, L0_conv_b_out)
    return x


_drawn_inputs = setup_inputs


def setup_inputs(seed=0):
    import zlib

    import numpy as np

    out = dict(_drawn_inputs(seed))
    spreads = {}
    factors = {'L0_conv_b_out': 2.851}
    for name, (base, spread) in spreads.items():
        noise = np.random.default_rng([zlib.crc32(name.encode()), seed]).standard_normal(out[name].shape)
        drawn = base * np.exp(spread * noise) if base else spread * noise
        out[name] = jnp.asarray(drawn.astype(out[name].dtype))
    for name, factor in factors.items():
        out[name] = (out[name] * factor).astype(out[name].dtype)
    return out
```

```python
from contextlib import ExitStack

import numpy as np

import concourse.bass as bass
from concourse import mybir

B, H, W, C = 16, 56, 56, 384
WS, HEADS, HD = 7, 12, 32
DISP = WS // 2
N = WS * WS
NW = W // WS
ROWS = B * (H // WS)
PAIRS = NW // 2
PT = 2 * N
RT = NW * N
PAD = 64
KC = C // 128
GROUPS = 32
GC = C // GROUPS
EPS = 1e-5
HH = HEADS // 2
TALL = WS - DISP
BIG = 1e30

SP_, SLABS, ST = 112, 4, 7
HALVES = 2 * SLABS
IMG_ROWS = H // WS
LAST = ROWS // 2 - 1

CONSTS = [("ident", 128), ("perm_in", 2 * PT), ("perm_out", 256), ("flip", 128), ("mask_rows", 512),
          ("pick", N), ("pick_scale", 2), ("mask", 4 * N), ("eye", N), ("same_window", 128),
          ("group", KC * GROUPS), ("mean_of", 128), ("ones", 128)]
CONST_AT, _at = {}, 0
for _name, _n in CONSTS:
    CONST_AT[_name] = (_at, _at + _n)
    _at += _n
CONST_COLS = _at
BIAS_K = 64 + N + 5


def place(kind, r, wc):
    if kind == 0:
        return r * 2 * WS + wc
    return wc * TALL + r if r < TALL else 2 * WS * TALL + wc * DISP + (r - TALL)


def constants():
    t = {n: np.zeros((128, k), np.float32) for n, k in CONSTS}
    t["ident"][:] = np.eye(128)
    pin = t["perm_in"].reshape(128, 2, PT)
    pout = t["perm_out"].reshape(128, 2, 128)
    for kind in range(2):
        for r in range(WS):
            for wc in range(2 * WS):
                w, c = divmod(wc, WS)
                pin[place(kind, r, wc), kind, w * N + r * WS + c] = 1
                pout[w * PAD + r * WS + c, kind, place(kind, r, wc)] = 1
        pads = [w * PAD + i for w in range(2) for i in range(N, PAD)]
        for n, p in enumerate(pads):
            pout[p, kind, PT + n] = 1
    tok = np.arange(N)
    low, right = tok // WS >= TALL, tok % WS >= TALL
    for w in range(2):
        t["flip"][N - 1 - tok, w * PAD + tok] = 1
        t["eye"][w * PAD + tok, tok] = 1
    t["pick"][N - 1 - tok, tok] = 1
    t["pick"][64 + N - 1 - tok, tok] = 1
    m0 = 64 + N
    t["pick"][m0] = BIG
    t["pick"][m0 + 1], t["pick"][m0 + 2] = BIG * right, BIG * ~right
    t["pick"][m0 + 3], t["pick"][m0 + 4] = BIG * low, BIG * ~low
    t["pick_scale"][:m0, 0] = 1
    t["pick_scale"][m0:, 1] = 1
    rows = t["mask_rows"].reshape(128, 4, 2, PAD)
    mask = t["mask"].reshape(2, PAD, 4, N)
    for bottom in range(2):
        for edge in range(2):
            kind = 2 * bottom + edge
            rows[m0, kind, :, N:] = -1
            if edge:
                rows[m0 + 1, kind, 1, :N] = -1.0 * ~right
                rows[m0 + 2, kind, 1, :N] = -1.0 * right
                mask[1, :N, kind] -= BIG * (right[:, None] != right[None, :])
            if bottom:
                rows[m0 + 3, kind, :, :N] = -1.0 * ~low
                rows[m0 + 4, kind, :, :N] = -1.0 * low
                mask[:, :N, kind] -= BIG * (low[:, None] != low[None, :])
    half = np.arange(128) // PAD
    t["same_window"][:] = -1.0 * (half[:, None] == half[None, :])
    ch = np.arange(C).reshape(KC, 128).T
    t["group"][:] = (ch[:, :, None] // GC == np.arange(GROUPS)).reshape(128, -1)
    t["mean_of"][:] = 1.0 / (SP_ * HALVES)
    t["ones"][:] = 1.0
    return np.concatenate([t[n] for n, _ in CONSTS], axis=1)


def need(eng, sem, value):
    if isinstance(value, int) and value <= 0:
        return
    eng.wait_ge(sem, value)


FILL = [([("q", 0), ("k", 0)], [("q", 1)]),
        ([("k", 1), ("q", 2)], [("k", 2)]),
        ([("v", 0)], [("v", 1)]),
        ([("v", 2), ("v", 3)], [("x", 0), ("x", 1), ("x", 2)])]
STAT = {6: ("mean", 0), 7: ("var", 0)}
STAT_KINDS = ("mean", "var")
FZ, FZ_VAR = 15, 7
BS_MADE, SC_MADE = 13, 18
BN_AT = [6, 6, 6, 6, 4, 4, 0, 0]


def step_units(k):
    first, second = FILL[k % 4]
    return first + ([STAT[k]] if k in STAT else []), second


UNITS = sum(len(a) + len(b) for a, b in map(step_units, range(8)))
PRO_UNITS = 12 + 2 + 2 + 3 + 13


def unit_at(k, kind, i):
    n = sum(len(a) + len(b) for a, b in map(step_units, range(k)))
    a, b = step_units(k)
    return n + (a + b).index((kind, i))


ROW_FIRST = PRO_UNITS - 13


def v_unit(n, odd, p):
    if isinstance(n, int) and n == 0 and odd == 0:
        return ROW_FIRST + 6 + p
    k = (0 if odd else 4) + (2 if p < 2 else 3)
    return PRO_UNITS + UNITS * (n if odd else n - 1) + unit_at(k, "v", p)


def build(nc, x, w_qkv, pos, w_out, b_out, const, y):
    fp32, f16, bf16, i32 = mybir.dt.float32, mybir.dt.float16, mybir.dt.bfloat16, mybir.dt.int32
    ALU, ACT, AX = mybir.AluOpType, mybir.ActivationFunctionType, mybir.AxisListType
    RMAX = bass.bass_isa.ReduceOp.max

    xt = x.rearrange("b h (e s) c -> b (h e) s c", s=SLABS * ST)

    ctx = ExitStack()
    with ctx:
        def sb(name, shape, dt):
            return ctx.enter_context(nc.sbuf_tensor(name, shape, dt))

        def sem(name):
            return ctx.enter_context(nc.semaphore(name))

        cst = sb("cst", [128, CONST_COLS], fp32)

        def const_of(name, rows=128):
            a, b = CONST_AT[name]
            return cst[0:rows, a:b]

        ident = const_of("ident")
        perm_in = const_of("perm_in", PT).rearrange("p (k n) -> p k n", k=2)
        perm_out = const_of("perm_out").rearrange("p (k n) -> p k n", k=2)
        mask_c = const_of("mask").rearrange("p (k n) -> p k n", k=4)
        group = const_of("group").rearrange("p (c g) -> p c g", c=KC)

        wnat = sb("wnat", [128, 9, C], fp32)
        wonat = sb("wonat", [128, 3, C], fp32)
        wh = sb("wh", [128, KC, 3 * C], f16)
        wl = sb("wl", [128, KC, 3 * C], f16)
        woh = sb("woh", [128, KC, C], f16)
        wol = sb("wol", [128, KC, C], f16)
        brow = sb("brow", [1, C], fp32)
        bout = sb("bout", [PT, C], fp32)
        amax = sb("amax", [128, 3], fp32)
        gmax = sb("gmax", [128, 3], fp32)
        p2 = sb("p2", [128, 3], fp32)
        sg = sb("sg", [128, 3], fp32)
        sc = sb("sc", [128, 8], fp32)
        bn = sb("bn", [128, N], fp32)
        bs = sb("bs", [128, N], fp32)
        bd = sb("bd", [128, N], fp32)
        bhi = sb("bhi", [128, N], f16)
        blo = sb("blo", [128, N], f16)
        bt = sb("bt", [128, 4, 128], f16)
        rb = sb("rb", [128, HH, N], bf16)
        rscale = sb("rscale", [128, 1], fp32)
        bc = sb("bc", [128, 4, N], fp32)
        blk = sb("blk", [128, 128], bf16)
        sx = sb("sx", [SP_, ST, C], fp32)
        st6 = sb("st6", [SP_, SLABS, GROUPS, 6], fp32)
        red1 = sb("red1", [SP_, GROUPS], fp32)
        red2 = sb("red2", [SP_, GROUPS], fp32)
        red3 = sb("red3", [SP_, GROUPS], fp32)
        red4 = sb("red4", [SP_, GROUPS], fp32)
        dev = sb("dev", [SP_, SLABS, 2, GROUPS], fp32)
        dev2 = sb("dev2", [SP_, SLABS, 2, GROUPS], fp32)
        meanb = sb("meanb", [128, GROUPS], fp32)
        varb = sb("varb", [128, GROUPS], fp32)
        root_v = sb("root_v", [128, GROUPS], fp32)
        rs0 = sb("rs0", [128, GROUPS], fp32)
        rs1 = sb("rs1", [128, GROUPS], fp32)
        rs2 = sb("rs2", [128, GROUPS], fp32)
        rs3 = sb("rs3", [128, GROUPS], fp32)
        spread = sb("spread", [128, KC, GROUPS], fp32)
        spread2 = sb("spread2", [128, KC, GROUPS], fp32)
        coef = sb("coef", [128, B + 2, 2 * KC], fp32)
        xs = sb("xs", [PT, 2, PAIRS, C], fp32)
        xb = sb("xb", [PT, 8, C], fp32)
        xn = sb("xn", [128, 2, NW, N], fp32)
        xh = sb("xh", [128, 2, KC, NW, PAD], f16)
        xl = sb("xl", [128, 2, KC, NW, PAD], f16)
        qkh = sb("qkh", [128, 6, RT], f16)
        qkl = sb("qkl", [128, 6, RT], f16)
        qst = sb("qst", [96, 2, 4, KC, RT], f16)
        kst = sb("kst", [96, 2, 4, KC, RT], f16)
        vh = sb("vh", [128, 2, PAIRS, HEADS, HD + 1], f16)
        vl = sb("vl", [128, 2, PAIRS, HEADS, HD], f16)
        lg = sb("lg", [128, 2, HH, N], fp32)
        mx = sb("mx", [128, 2, HEADS], fp32)
        m2 = sb("m2", [128, 2, 2, HEADS], bf16)
        dm = sb("dm", [128, 2, 2 * HEADS, N], bf16)
        pf = sb("pf", [128, HEADS, N], fp32)
        ph = sb("ph", [128, HEADS, 2 * PAD], f16)
        pl = sb("pl", [128, HEADS, 2 * PAD], f16)
        rv = sb("rv", [128, HEADS], fp32)
        av = sb("av", [128, HEADS, HD], fp32)
        ath = sb("ath", [128, KC, PT], f16)
        atl = sb("atl", [128, KC, PT], f16)

        ps_sa = ctx.enter_context(nc.psum_tensor("ps_sa", [128, 2, 512], fp32))
        ps_st = ctx.enter_context(nc.psum_tensor("ps_st", [128, 2, 512], fp32))
        ps_pv = ctx.enter_context(nc.psum_tensor("ps_pv", [128, 512], fp32))
        ps_post = ctx.enter_context(nc.psum_tensor("ps_post", [128, 512], fp32))
        ps_pj = [ctx.enter_context(nc.psum_tensor(f"ps_pj{i}", [128, 512], fp32)) for i in range(2)]
        pv_out = ps_pv[:, 0:HEADS * (HD + 1)].rearrange("p (h d) -> p h d", h=HEADS)
        at_out = ps_post[:, 0:KC * 128].rearrange("p (c n) -> p c n", c=KC)

        s_const = sem("const_loaded")
        s_init = sem("buffers_set")
        s_zero = sem("score_banks_zeroed")
        s_cast = sem("tables_cast")
        s_pre = sem("scalars_made")
        s_gmax = sem("maxima_spread")
        s_bias = sem("bias_tables_made")
        s_slab = sem("slab_loaded")
        s_bn = sem("slab_measured")
        s_fz = sem("statistics_step")
        s_pow = sem("variance_rooted")
        s_reached = sem("sp_waits_met")
        s_coef = sem("coefficients_made")
        s_load = [sem("row_loaded_even"), sem("row_loaded_odd")]
        s_stack = [sem("stacks_filled_even"), sem("stacks_filled_odd")]
        s_store = [sem(f"pair_stored_{i}") for i in range(8)]
        s_pj = sem("unit_in_psum")
        s_pjr = sem("unit_taken")
        s_hi = sem("high_part_written")
        s_xh = sem("x_high_written")
        s_xl = sem("x_low_written")
        s_xb = sem("residual_made")
        s_sa = sem("scores_in_psum")
        s_lg = sem("logits_made")
        s_mx = sem("maxima_made")
        s_mh = sem("maxima_high")
        s_ml = sem("maxima_low")
        s_dm = sem("shift_tables_made")
        s_st = sem("transposed_scores_in_psum")
        s_ph = sem("probabilities_high")
        s_pl = sem("probabilities_low")
        s_pv = sem("attended_in_psum")
        s_rv = sem("sums_inverted")
        s_av = sem("attended_normalized")
        s_at = sem("attended_transposed")
        s_ah = sem("attended_high")
        s_al = sem("attended_low")
        s_out = sem("output_in_psum")
        s_fin = sem("output_made")

        STACK = 24 * 16
        LOADS = (2 * 3 + 4) * 16
        STORES = [32, 32, 32, 64]

        def unit_count(n, k, kind, i):
            return PRO_UNITS + UNITS * n + unit_at(k, kind, i) + 1

        def hi_index(n, k, kind, i):
            before = 10 + 20 * n + 10 * (k // 4)
            flat = [u for a, b in FILL for u in a + b if u[0] != "x"]
            return before + flat.index((kind, i))

        def x_units(n, k, c):
            return 6 + 6 * n + 3 * (k // 4) + c

        def x_free(n, odd):
            if isinstance(n, int) and n == 0 and not odd:
                return ROW_FIRST + 10
            return unit_count(n if odd else n - 1, 3 if odd else 7, "v", PAIRS - 1)

        def move_row(eng, dram_, tile_of, sems, pair, load, at):
            na, nb = TALL, DISP
            image, row_a, row_b = at
            dram = dram_[image]
            split = 2 * WS * na
            pieces = []
            if pair < PAIRS - 1:
                c0 = 2 * WS * pair + DISP
                pieces.append((0, split, dram[bass.ds(row_a, na), c0:c0 + 2 * WS, :]))
                pieces.append((split, PT, dram[bass.ds(row_b, nb), c0:c0 + 2 * WS, :]))
            else:
                c0, k = 2 * WS * pair + DISP, 2 * WS - DISP
                pieces.append((0, k * na, dram[bass.ds(row_a, na), c0:W, :].rearrange("r c f -> c r f")))
                pieces.append((k * na, split, dram[bass.ds(row_a, na), 0:DISP, :].rearrange("r c f -> c r f")))
                pieces.append((split, split + k * nb, dram[bass.ds(row_b, nb), c0:W, :].rearrange("r c f -> c r f")))
                pieces.append((split + k * nb, PT, dram[bass.ds(row_b, nb), 0:DISP, :].rearrange("r c f -> c r f")))
            for a, b, d in pieces:
                t = tile_of[a:b]
                if load:
                    eng.dma_start(t, d).then_inc(sems, 16)
                else:
                    eng.dma_start(d, t).then_inc(sems, 16)

        def rows_of(n, odd):
            first = 2 * WS * (n & 3) + WS * odd
            after = 2 * WS * ((n + 1) & 3) if odd else first + WS
            return (n >> 2) & (B - 1), first + DISP, after

        def bias_kind(n, odd, pair):
            edge = 1 if pair == PAIRS - 1 else 0
            if not odd:
                return edge
            return (((n & 3) + 1) >> 2) * 2 + edge

        block = ctx.enter_context(nc.Block())

        @block.sync
        def _(sp):
            sp.dma_start(cst[:, :], const[:, :]).then_inc(s_const, 16)
            sp.dma_start(wnat[:, :, :], w_qkv.rearrange("(a p) c -> p a c", p=128)).then_inc(s_const, 16)
            sp.dma_start(wonat[:, :, :], w_out.rearrange("(a p) c -> p a c", p=128)).then_inc(s_const, 16)
            sp.dma_start(brow[:, :], b_out.rearrange("(a c) -> a c", a=1)).then_inc(s_const, 16)
            def slab(img, s):
                sp.dma_start(sx[:, :, :], xt[img, :, s * ST:(s + 1) * ST, :]).then_inc(s_slab, 16)
            slab(0, 0)
            sp.wait_ge(s_init, 1)
            for r in range(WS):
                for c in range(WS):
                    for at in (0, 64):
                        q = at + r * WS + c
                        sp.dma_start(bn[q:q + 1, :].rearrange("p (r c) -> p r c", r=WS),
                                     pos[r:r + WS, c:c + WS].rearrange("(a r) c -> a r c", a=1)).then_inc(s_const, 16)
            def load_row(n, odd):
                at = rows_of(n, odd)
                for p in range(PAIRS):
                    move_row(sp, x, xs[:, odd, p, :], s_load[odd], p, True, at)
            load_row(0, 0)
            load_row(0, 1)
            for s in range(1, SLABS):
                sp.wait_ge(s_bn, s)
                slab(0, s)
            sp.wait_ge(s_bn, SLABS)
            slab(1, 0)
            sp.wait_ge(s_bn, SLABS + 1)
            slab(1, 1)

            def reach(sem, value):
                if not (isinstance(value, int) and value <= 0):
                    sp.wait_ge(sem, value)
                    sp.sem_inc(s_reached, 1)

            def stack_row(b, done_units, free):
                reach(s_pjr, done_units)
                reach(s_st, free)
                for part, (qp, kp) in enumerate(((qkh, qkh), (qkl, qkh), (qkh, qkl))):
                    for g in range(4):
                        rows = slice(32 * g, 32 * g + 32)
                        to = slice(32 * part, 32 * part + 32)
                        sp.dma_start(qst[to, b, g, :, :], qp[rows, 0:KC, :]).then_inc(s_stack[b], 16)
                        sp.dma_start(kst[to, b, g, :, :], kp[rows, KC:2 * KC, :]).then_inc(s_stack[b], 16)

            stack_row(0, ROW_FIRST + 6, 0)

            def step(n, first=False, last=False):
                for k in range(8):
                    odd, p, t = k // 4, k % 4, 8 * n + k
                    if p == 1 and not last:
                        reach(s_xb, 8 * n + 4 * odd + 4)
                        reach(s_pj, ROW_FIRST + 13 if first and odd else
                             (ROW_FIRST if first else unit_count(n - 1, 4 * odd + 3, "x", 2)))
                        load_row(n + 1, odd)
                    if p == 2 and not (last and odd):
                        stack_row(1 - odd, unit_count(n, 4 * odd + 1, "k", 2), 8 * n + 4 * odd)
                    if k == 6 and not last:
                        m = n + 2
                        reach(s_bn, SLABS + 2 + n)
                        slab_at = (m & 3) * ST
                        img = ((m >> 2) + 1) & (B - 1)
                        sp.dma_start(sx[:, :, :], xt[img, :, bass.ds(slab_at, ST), :]).then_inc(s_slab, 16)
                    if not (first and k < 3):
                        store(t - 3, n, k - 3)

            def store(t, n, j):
                reach(s_fin, t + 1)
                if j < 0:
                    n, j = n - 1, j + 8
                at = rows_of(n, j // 4)
                move_row(sp, y, xb[:, j, :], s_store[j], j % 4, False, at)

            step(0, first=True)
            with nc.sync.Fori(1, LAST) as n:
                step(n)
            step(LAST, last=True)
            for j in range(5, 8):
                store(8 * LAST + j, LAST, j)
            for j in range(8):
                sp.wait_ge(s_store[j], STORES[j % 4] * (LAST + 1))

        @block.gpsimd
        def _(pool):
            nc.gpsimd.memset(bn[:, :], 0.0).then_inc(s_init, 1)
            nc.gpsimd.memset(xh[:, :, :, :, :], 0.0).then_inc(s_init, 1)
            nc.gpsimd.memset(xl[:, :, :, :, :], 0.0).then_inc(s_init, 1)
            nc.gpsimd.memset(vh[:, :, :, :, :], 1.0).then_inc(s_init, 1)
            nc.gpsimd.memset(ph[:, :, :], 0.0).then_inc(s_init, 1)
            nc.gpsimd.memset(pl[:, :, :], 0.0).then_inc(s_init, 1)
            pool.wait_ge(s_init, 5)
            for w in range(2):
                nc.gpsimd.memset(ph[:, :, w * PAD + N:(w + 1) * PAD], 1.0).then_inc(s_init, 1)
            pool.wait_ge(s_pre, 3)
            nc.gpsimd.partition_all_reduce(gmax[:, :], amax[:, :], 128, RMAX).then_inc(s_gmax, 1)

            def x_low(unit, index, slot, b, c, used):
                pool.wait_ge(s_pjr, unit)
                pool.wait_ge(s_xh, index + 1)
                need(pool, s_pj, used)
                nc.gpsimd.tensor_tensor(xl[:, b, c, :, 0:N], xn[:, slot, :, :], xh[:, b, c, :, 0:N],
                                        ALU.subtract).then_inc(s_xl, 1)

            def residual(t, n, j, first=False):
                if j >= 8:
                    n, j = n + 1, j - 8
                pool.wait_ge(s_load[j // 4], LOADS * (n + 1))
                need(pool, s_store[j], STORES[j % 4] * n)
                nc.gpsimd.tensor_tensor(xb[:, j, :], xs[:, j // 4, j % 4, :], bout[:, :], ALU.add).then_inc(s_xb, 1)

            for c in range(KC):
                x_low(ROW_FIRST - KC + c + 1, c, c % 2, 0, c, 0)
            for c in range(KC):
                x_low(PRO_UNITS - KC + c + 1, KC + c, (KC + c) % 2, 1, c, 0)
            pool.wait_ge(s_pjr, 14)
            for j in range(3):
                residual(j, 0, j)

            def step(n, first=False, last=False):
                for k in range(8):
                    t = 8 * n + k
                    if not (last and k + 3 >= 8):
                        residual(t + 3, n, k + 3, first)
                    pool.wait_ge(s_ml, t + 1)
                    need(pool, s_st, t - 1)
                    nc.gpsimd.tensor_tensor(
                        dm[:, k % 2, :, :],
                        const_of("eye").unsqueeze(1).broadcast_to([128, 2 * HEADS, N]),
                        m2[:, k % 2, :, :].rearrange("p a h -> p (a h)").unsqueeze(2).broadcast_to([128, 2 * HEADS, N]),
                        ALU.mult).then_inc(s_dm, 1)
                    if k % 4 == 3 and not last:
                        for c in range(KC):
                            x_low(unit_count(n, k, "x", c), x_units(n, k, c), (k // 4 + c) % 2, k // 4, c,
                                  x_free(n, k // 4))

            step(0, first=True)
            with nc.gpsimd.Fori(1, LAST) as n:
                step(n)
            step(LAST, last=True)

        @block.scalar
        def _(act):
            def high(unit, kind, i, b, p_free, stack_sem, stack_need, bank):
                act.wait_ge(s_pj, unit)
                if kind == "v":
                    need(act, s_pv, p_free)
                    nc.scalar.activation(vh[:, b, i, :, 0:HD], ps_pj[bank][:, 0:C].rearrange("p (h d) -> p h d", h=HEADS),
                                         ACT.Copy).then_inc(s_hi, 1)
                else:
                    need(act, stack_sem, stack_need)
                    nc.scalar.activation(qkh[:, (KC if kind == "k" else 0) + i, :], ps_pj[bank][:, 0:RT],
                                         ACT.Copy).then_inc(s_hi, 1)

            def x_high(unit, slot, b, c, used):
                act.wait_ge(s_pjr, unit)
                need(act, s_pj, used)
                nc.scalar.activation(xh[:, b, c, :, 0:N], xn[:, slot, :, :], ACT.Copy).then_inc(s_xh, 1)

            def root(count):
                act.wait_ge(s_fz, count)
                nc.scalar.activation(root_v[:, :], varb[:, :], ACT.Sqrt).then_inc(s_pow, 1)

            act.wait_ge(s_init, 8)
            root(FZ_VAR)
            for c in range(KC):
                x_high(ROW_FIRST - KC + c + 1, c % 2, 0, c, 0)
            u = ROW_FIRST
            for kind, i in [v for a, b in FILL for v in a + b]:
                if kind == "x":
                    x_high(u + 1, (KC + i) % 2, 1, i, 0)
                else:
                    high(u + 1, kind, i, 0, 0, None, 0, u % 2)
                u += 1

            def units(n, k, part, first, last):
                base = PRO_UNITS + UNITS * n
                odd = k // 4
                for kind, i in step_units(k)[part]:
                    j = unit_at(k, kind, i)
                    if kind in STAT_KINDS:
                        continue
                    if kind == "x":
                        x_high(base + j + 1, (odd + i) % 2, odd, i, x_free(n, odd))
                    else:
                        high(base + j + 1, kind, i, 1 - odd, 8 * n + 4 * odd - 4 + i + 1,
                             s_stack[odd], STACK * (n + 1), j % 2)

            def step(n, first=False, last=False):
                for k in range(8):
                    t = 8 * n + k
                    if not (first and k < 3):
                        attended_high(t - 3)
                    if not (last and k >= 4):
                        units(n, k, 0, first, last)
                    if not (first and k < 1):
                        probabilities(t - 1)
                    if not (last and (k >= 4 or k == 3)):
                        units(n, k, 1, first, last)
                    if k == 7 and not last:
                        root(FZ * (n + 1) + FZ_VAR)

            def attended_high(t):
                act.wait_ge(s_at, t + 1)
                need(act, s_out, t)
                nc.scalar.activation(ath[:, :, :], at_out[:, :, 0:PT], ACT.Copy).then_inc(s_ah, 1)

            def probabilities(t):
                act.wait_ge(s_st, t + 1)
                need(act, s_pl, t)
                nc.scalar.activation(pf[:, :, :].rearrange("p (a h) n -> p a (h n)", a=2), ps_st[:, :, 0:HH * N], ACT.Exp,
                                     scale=sc[:, 0:1])
                need(act, s_pv, t)
                for w in range(2):
                    rows = slice(w * PAD, (w + 1) * PAD)
                    e = nc.scalar.activation(
                        ph[rows, :, w * PAD:w * PAD + N].rearrange("p (a h) n -> p a h n", a=2),
                        ps_st[rows, :, 0:HH * N].rearrange("p a (h n) -> p a h n", h=HH), ACT.Exp, scale=sc[rows, 0:1])
                e.then_inc(s_ph, 1)

            act.wait_ge(s_pre, SC_MADE)
            step(0, first=True)
            with nc.scalar.Fori(1, LAST) as n:
                step(n)
            step(LAST, last=True)
            end = 8 * (LAST + 1)
            attended_high(end - 3)
            probabilities(end - 1)
            attended_high(end - 2)
            attended_high(end - 1)

        @block.vector
        def _(dve):
            made = [0]

            def pre(ins):
                made[0] += 1
                ins.then_inc(s_pre, 1)
                dve.wait_ge(s_pre, made[0])

            nc.vector.memset(ps_sa[:, :, :], 0.0).then_inc(s_zero, 1)
            dve.wait_ge(s_const, 16 * (4 + 2 * N))
            nc.vector.tensor_reduce(amax[:, 0:1], wnat[:, :, :], AX.XY, ALU.max, apply_absolute_value=True).then_inc(s_pre, 1)
            nc.vector.tensor_reduce(amax[:, 1:2], wonat[:, :, :], AX.XY, ALU.max, apply_absolute_value=True).then_inc(s_pre, 1)
            nc.vector.tensor_reduce(amax[:, 2:3], bn[:, :], AX.X, ALU.max, apply_absolute_value=True).then_inc(s_pre, 1)
            made[0] = 3
            dve.wait_ge(s_gmax, 1)
            pre(nc.vector.tensor_scalar(gmax[:, 0:2], gmax[:, 0:2], 2.0 ** -20, None, ALU.max))
            pre(nc.vector.tensor_scalar(p2[:, 0:2].bitcast(i32), gmax[:, 0:2].bitcast(i32), 0x7F800000, None, ALU.bitwise_and))
            pre(nc.vector.reciprocal(sg[:, 0:2], p2[:, 0:2]))
            pre(nc.vector.scalar_tensor_tensor(sc[:, 0:1], p2[:, 0:1], HD ** -0.5, p2[:, 0:1], ALU.mult, ALU.mult))
            pre(nc.vector.scalar_tensor_tensor(sc[:, 1:2], sg[:, 0:1], HD ** 0.5, sg[:, 0:1], ALU.mult, ALU.mult))
            pre(nc.vector.tensor_tensor(sc[:, 2:3], p2[:, 0:1], p2[:, 1:2], ALU.mult))
            pre(nc.vector.tensor_scalar(gmax[:, 2:3], gmax[:, 2:3], sc[:, 1:2], 2.0 ** -60, ALU.mult, ALU.max))
            pre(nc.vector.tensor_scalar(p2[:, 2:3].bitcast(i32), gmax[:, 2:3].bitcast(i32), 0x7F800000, None, ALU.bitwise_and))
            pre(nc.vector.reciprocal(sg[:, 2:3], p2[:, 2:3]))
            pre(nc.vector.tensor_scalar(bs[:, :], bn[:, :], sc[:, 1:2], None, ALU.mult))
            assert made[0] == BS_MADE
            pre(nc.vector.tensor_scalar(bd[:, :], bs[:, :], sg[:, 2:3], None, ALU.mult))
            pre(nc.vector.tensor_copy(bhi[:, :], bd[:, :]))
            pre(nc.vector.tensor_tensor(blo[:, :], bd[:, :], bhi[:, :], ALU.subtract))
            pre(nc.vector.tensor_copy(bt[:, :, :].rearrange("p a b -> p (a b)"), const_of("mask_rows")))
            for w in range(2):
                cols = slice(w * PAD, w * PAD + N)
                for part, at in ((bhi, 0), (blo, 64)):
                    nc.vector.tensor_copy(bt[at:at + N, :, cols],
                                          part[at:at + N, :].unsqueeze(1).broadcast_to([N, 4, N])).then_inc(s_bias, 1)
            ps_ = const_of("pick_scale")
            pre(nc.vector.scalar_tensor_tensor(rscale[:, :], ps_[:, 0:1], p2[:, 2:3], ps_[:, 1:2], ALU.mult, ALU.add))
            nc.vector.tensor_scalar(rb[:, :, :], const_of("pick").unsqueeze(1).broadcast_to([128, HH, N]),
                                    rscale[:, 0:1], None, ALU.mult).then_inc(s_bias, 1)
            nc.vector.tensor_copy(blk[:, :], const_of("same_window")).then_inc(s_bias, 1)
            assert made[0] == SC_MADE

            u = 0
            for kind in ("w", "o"):
                for c in range(KC):
                    for a in range(3 if kind == "w" else 1):
                        hi_, lo_ = (wh, wl) if kind == "w" else (woh, wol)
                        s = sg[:, 0:1] if kind == "w" else sg[:, 1:2]
                        cols = slice(a * C, (a + 1) * C)
                        dve.wait_ge(s_pj, u + 1)
                        nc.vector.tensor_scalar(hi_[:, c, cols], ps_pj[u % 2][:, 0:C], s, None, ALU.mult).then_inc(s_cast, 1)
                        dve.wait_ge(s_cast, u + 1)
                        nc.vector.scalar_tensor_tensor(lo_[:, c, cols], ps_pj[u % 2][:, 0:C], s, hi_[:, c, cols],
                                                       ALU.mult, ALU.subtract).then_inc(s_pjr, 1)
                        u += 1
            dve.wait_ge(s_pj, u + 1)
            nc.vector.tensor_tensor(bc[:, :, :], mask_c, ps_pj[u % 2][:, 0:N].unsqueeze(1).broadcast_to([128, 4, N]),
                                    ALU.add).then_inc(s_pjr, 1)
            u += 1
            dve.wait_ge(s_pj, u + 1)
            nc.vector.tensor_copy(bout[:, :], ps_pj[u % 2][0:PT, 0:C]).then_inc(s_pjr, 1)
            u += 1

            def measure(slab_slot, groups, done):
                for g in groups:
                    last = nc.vector.bn_stats(st6[:, slab_slot, g, :], sx[:, :, g * GC:(g + 1) * GC])
                if done:
                    last.then_inc(s_bn, 1)

            def stat_sums():
                nc.vector.tensor_reduce(red1[:, :], st6[:, :, :, 1:5:3].rearrange("p s g e -> p g s e"), AX.XY,
                                        ALU.add).then_inc(s_fz, 1)
                nc.vector.tensor_reduce(red2[:, :], st6[:, :, :, 2:6:3].rearrange("p s g e -> p g s e"), AX.XY,
                                        ALU.add).then_inc(s_fz, 1)

            def stat_mean(unit, bank, base):
                dve.wait_ge(s_pj, unit)
                nc.vector.tensor_copy(meanb[:, :], ps_pj[bank][:, 0:GROUPS]).then_inc(s_pjr, 1)
                dve.wait_ge(s_pjr, unit)
                nc.vector.tensor_tensor(dev[:, :, :, :], st6[:, :, :, 1:5:3].rearrange("p s g e -> p s e g"),
                                        meanb[0:SP_, :].unsqueeze(1).unsqueeze(1).broadcast_to([SP_, SLABS, 2, GROUPS]),
                                        ALU.subtract).then_inc(s_fz, 1)
                dve.wait_ge(s_fz, base + 3)
                nc.vector.tensor_tensor(dev2[:, :, :, :], dev[:, :, :, :], dev[:, :, :, :], ALU.mult).then_inc(s_fz, 1)
                dve.wait_ge(s_fz, base + 4)
                nc.vector.tensor_reduce(red3[:, :], dev2[:, :, :, :].rearrange("p s e g -> p g (s e)"), AX.X,
                                        ALU.add).then_inc(s_fz, 1)
                dve.wait_ge(s_fz, base + 5)
                nc.vector.scalar_tensor_tensor(red4[:, :], red2[:, :], 2.0 / (ST * GC), red3[:, :], ALU.mult,
                                               ALU.add).then_inc(s_fz, 1)

            def stat_var(unit, bank):
                dve.wait_ge(s_pj, unit)
                nc.vector.tensor_scalar(varb[:, :], ps_pj[bank][:, 0:GROUPS], EPS, None, ALU.add).then_inc(s_pjr, 1)
                dve.wait_ge(s_pjr, unit)
                nc.vector.tensor_copy(rs2[:, :], varb[:, :]).then_inc(s_fz, 1)

            def stat_coef(slot, base, roots):
                dve.wait_ge(s_pow, roots)
                nc.vector.reciprocal(rs0[:, :], root_v[:, :]).then_inc(s_fz, 1)
                nc.vector.tensor_tensor(spread[:, :, :], group, meanb[:, :].unsqueeze(1).broadcast_to([128, KC, GROUPS]),
                                        ALU.mult).then_inc(s_fz, 1)
                dve.wait_ge(s_fz, base + 8)
                nc.vector.tensor_tensor(rs1[:, :], rs0[:, :], rs0[:, :], ALU.mult).then_inc(s_fz, 1)
                dve.wait_ge(s_fz, base + 9)
                nc.vector.tensor_reduce(coef[:, slot, 0:KC], spread[:, :, :], AX.X, ALU.add).then_inc(s_fz, 1)
                dve.wait_ge(s_fz, base + 10)
                nc.vector.tensor_tensor(rs2[:, :], rs1[:, :], varb[:, :], ALU.mult).then_inc(s_fz, 1)
                dve.wait_ge(s_fz, base + 12)
                nc.vector.tensor_scalar(rs1[:, :], rs2[:, :], -0.5, 1.5, ALU.mult, ALU.add).then_inc(s_fz, 1)
                dve.wait_ge(s_fz, base + 13)
                nc.vector.tensor_tensor(rs3[:, :], rs1[:, :], rs0[:, :], ALU.mult).then_inc(s_fz, 1)
                dve.wait_ge(s_fz, base + 14)
                nc.vector.tensor_tensor(spread2[:, :, :], group, rs3[:, :].unsqueeze(1).broadcast_to([128, KC, GROUPS]),
                                        ALU.mult).then_inc(s_fz, 1)
                dve.wait_ge(s_fz, base + 15)
                nc.vector.tensor_reduce(coef[:, slot, KC:2 * KC], spread2[:, :, :], AX.X, ALU.add).then_inc(s_coef, 1)

            for s in range(SLABS):
                dve.wait_ge(s_slab, 16 * (s + 1))
                measure(s, range(GROUPS), True)
            dve.wait_ge(s_bn, SLABS)
            stat_sums()
            stat_mean(u + 1, u % 2, 0)
            stat_var(u + 2, (u + 1) % 2)
            stat_coef(0, 0, 1)
            u += 2
            dve.wait_ge(s_slab, 16 * (SLABS + 1))
            measure(0, range(GROUPS), True)
            dve.wait_ge(s_coef, 1)

            def x_norm(unit, bank, index, slot, img, c):
                dve.wait_ge(s_pj, unit)
                need(dve, s_xh, index - 1)
                need(dve, s_xl, index - 1)
                nc.vector.tensor_scalar(xn[:, slot, :, :].rearrange("p w n -> p (w n)"), ps_pj[bank][:, 0:RT],
                                        coef[:, img, c:c + 1], coef[:, img, KC + c:KC + c + 1],
                                        ALU.subtract, ALU.mult).then_inc(s_pjr, 1)

            def low(bank, hi, kind, i, b, p_free, stack_sem, stack_need):
                dve.wait_ge(s_hi, hi)
                if kind == "v":
                    need(dve, s_pv, p_free)
                    nc.vector.tensor_tensor(vl[:, b, i, :, :], ps_pj[bank][:, 0:C].rearrange("p (h d) -> p h d", h=HEADS),
                                            vh[:, b, i, :, 0:HD], ALU.subtract).then_inc(s_pjr, 1)
                else:
                    need(dve, stack_sem, stack_need)
                    a = (KC if kind == "k" else 0) + i
                    nc.vector.tensor_tensor(qkl[:, a, :], ps_pj[bank][:, 0:RT], qkh[:, a, :], ALU.subtract).then_inc(s_pjr, 1)

            for c in range(KC):
                x_norm(u + 1, u % 2, c, c % 2, 0, c)
                u += 1
            h = 0
            for kind, i in [v for a, b in FILL for v in a + b]:
                if kind == "x":
                    x_norm(u + 1, u % 2, KC + i, (KC + i) % 2, 0, i)
                else:
                    low(u % 2, h + 1, kind, i, 0, 0, None, 0)
                    h += 1
                u += 1
            assert u == PRO_UNITS

            def units(n, k, part, first):
                base, odd = PRO_UNITS + UNITS * n, k // 4
                for kind, i in step_units(k)[part]:
                    j = unit_at(k, kind, i)
                    if kind == "x":
                        if i == 0:
                            dve.wait_ge(s_coef, n + 1)
                        x_norm(base + j + 1, j % 2, x_units(n, k, i), (odd + i) % 2, (n + 1) >> 2, i)
                    elif kind == "mean":
                        stat_mean(base + j + 1, j % 2, FZ * (n + 1))
                    elif kind == "var":
                        stat_var(base + j + 1, j % 2)
                    else:
                        low(j % 2, hi_index(n, k, kind, i) + 1, kind, i, 1 - odd,
                            8 * n + 4 * odd - 4 + i + 1, s_stack[odd], STACK * (n + 1))

            def logits(t, n, k):
                dve.wait_ge(s_sa, t + 1)
                bias = bc[:, bias_kind(n, k // 4, k % 4), :]
                nc.vector.tensor_tensor(lg[:, :, :, :], ps_sa[:, :, 0:HH * N].rearrange("p a (h n) -> p a h n", h=HH),
                                        bias.unsqueeze(1).unsqueeze(1).broadcast_to([128, 2, HH, N]),
                                        ALU.add).then_inc(s_lg, 1)

            def attended_low(t):
                dve.wait_ge(s_ah, t + 1)
                need(dve, s_out, t)
                nc.vector.tensor_tensor(atl[:, :, :], at_out[:, :, 0:PT], ath[:, :, :], ALU.subtract).then_inc(s_al, 1)

            def maxima(t, k):
                dve.wait_ge(s_lg, t + 1)
                nc.vector.tensor_reduce(mx[:, k % 2, :], lg[:, :, :, :].rearrange("p a h n -> p (a h) n"), AX.X,
                                        ALU.max).then_inc(s_mx, 1)

            def maxima_high(t, k):
                dve.wait_ge(s_mx, t + 1)
                need(dve, s_dm, t - 1)
                nc.vector.tensor_copy(m2[:, k % 2, 0, :], mx[:, k % 2, :]).then_inc(s_mh, 1)

            def maxima_low(t, k):
                dve.wait_ge(s_mh, t + 1)
                nc.vector.tensor_tensor(m2[:, k % 2, 1, :], mx[:, k % 2, :], m2[:, k % 2, 0, :], ALU.subtract).then_inc(s_ml, 1)

            def invert(t):
                dve.wait_ge(s_pv, t + 1)
                nc.vector.reciprocal(rv[:, :], pv_out[:, :, HD]).then_inc(s_rv, 1)

            def normalize(t):
                dve.wait_ge(s_rv, t + 1)
                need(dve, s_at, t)
                nc.vector.tensor_tensor(av[:, :, :], pv_out[:, :, 0:HD], rv[:, :].unsqueeze(2).broadcast_to([128, HEADS, HD]),
                                        ALU.mult).then_inc(s_av, 1)

            def output(t, j):
                dve.wait_ge(s_out, t + 1)
                dve.wait_ge(s_xb, t + 1)
                nc.vector.scalar_tensor_tensor(xb[:, j % 8, :], ps_post[0:PT, 0:C], sc[0:PT, 2:3], xb[:, j % 8, :],
                                               ALU.mult, ALU.add).then_inc(s_fin, 1)

            def split_probabilities(t):
                dve.wait_ge(s_ph, t + 1)
                need(dve, s_pv, t)
                for w in range(2):
                    rows, cols = slice(w * PAD, (w + 1) * PAD), slice(w * PAD, w * PAD + N)
                    e = nc.vector.tensor_tensor(pl[rows, :, cols], pf[rows, :, :], ph[rows, :, cols], ALU.subtract)
                e.then_inc(s_pl, 1)

            def step(n, first=False, last=False):
                at = 0
                for k in range(8):
                    t = 8 * n + k
                    logits(t, n, k)
                    if not (first and k < 3):
                        attended_low(t - 3)
                    maxima(t, k)
                    if not last and k == 0:
                        dve.wait_ge(s_slab, 16 * (SLABS + 2 + n))
                    if not last and BN_AT[k]:
                        measure((n + 1) & 3, range(at, at + BN_AT[k]), at + BN_AT[k] == GROUPS)
                        at += BN_AT[k]
                    maxima_high(t, k)
                    if not last and k == 6:
                        dve.wait_ge(s_bn, SLABS + 2 + n)
                        stat_sums()
                    if not (last and k >= 4):
                        units(n, k, 0, first)
                    maxima_low(t, k)
                    if not (first and k < 2):
                        invert(t - 2)
                        normalize(t - 2)
                    if not (first and k < 3):
                        output(t - 3, k - 3)
                    if not (first and k < 1):
                        split_probabilities(t - 1)
                    if not (last and (k >= 4 or k == 3)):
                        units(n, k, 1, first)
                    if not last and k == 7:
                        stat_coef(((n + 1) >> 2) + 1, FZ * (n + 1), n + 2)

            step(0, first=True)
            with nc.vector.Fori(1, LAST) as n:
                step(n)
            step(LAST, last=True)
            end = 8 * (LAST + 1)
            attended_low(end - 3)
            invert(end - 2)
            normalize(end - 2)
            output(end - 3, 5)
            split_probabilities(end - 1)
            attended_low(end - 2)
            invert(end - 1)
            normalize(end - 1)
            output(end - 2, 6)
            attended_low(end - 1)
            output(end - 1, 7)

        @block.tensor
        def _(pe):
            mm = nc.tensor.matmul

            def bank_free(unit):
                need(pe, s_pjr, unit - 2)

            pe.wait_ge(s_const, 16 * (4 + 2 * N))
            u = 0
            for kind in ("w", "o"):
                for c in range(KC):
                    for a in range(3 if kind == "w" else 1):
                        bank_free(u + 1)
                        for i in range(3):
                            src = wnat[:, 3 * a + i, :] if kind == "w" else wonat[:, i, :]
                            m = nc.tensor.transpose(ps_pj[u % 2][:, i * 128:(i + 1) * 128], src[:, c * 128:(c + 1) * 128], ident)
                        m.then_inc(s_pj, 1)
                        u += 1
            bank_free(u + 1)
            pe.wait_ge(s_pre, BS_MADE)
            mm(ps_pj[u % 2][:, 0:N], const_of("flip", N), bs[0:N, :], start=True, stop=True).then_inc(s_pj, 1)
            u += 1
            bank_free(u + 1)
            mm(ps_pj[u % 2][0:PT, 0:C], const_of("ones", 1)[:, 0:PT], brow[:, :], start=True, stop=True).then_inc(s_pj, 1)
            u += 1

            def stat_unit(kind, unit, bank, fz):
                bank_free(unit)
                pe.wait_ge(s_fz, fz)
                mm(ps_pj[bank][:, 0:GROUPS], const_of("mean_of", SP_), (red1 if kind == "mean" else red4)[:, :],
                   start=True, stop=True).then_inc(s_pj, 1)

            stat_unit("mean", u + 1, u % 2, 2)
            stat_unit("var", u + 2, (u + 1) % 2, 6)
            u += 2

            def x_unit(unit, bank, b, c, loaded):
                bank_free(unit)
                pe.wait_ge(s_load[b], loaded)
                for p in range(PAIRS):
                    m = nc.tensor.transpose(ps_pj[bank][:, p * PT:(p + 1) * PT], xs[:, b, p, c * 128:(c + 1) * 128],
                                            perm_in[:, 1 if p == PAIRS - 1 else 0, :])
                m.then_inc(s_pj, 1)

            def project_unit(unit, bank, kind, i, b, x_ready):
                bank_free(unit)
                pe.wait_ge(s_xh, x_ready)
                pe.wait_ge(s_xl, x_ready)
                for c in range(KC):
                    for n_, (xa, wa) in enumerate(((xh, wh), (xh, wl), (xl, wh))):
                        on = dict(start=c == 0 and n_ == 0, stop=c == KC - 1 and n_ == 2)
                        if kind == "v":
                            m = mm(ps_pj[bank][:, 0:C], xa[:, b, c, 2 * i:2 * i + 2, :].rearrange("p w n -> p (w n)"),
                                   wa[:, c, 2 * C:3 * C], **on)
                        else:
                            o = (C if kind == "k" else 0) + i * 128
                            m = mm(ps_pj[bank][:, 0:RT].rearrange("p (w n) -> p w n", w=NW), wa[:, c, o:o + 128],
                                   xa[:, b, c, :, 0:N], **on)
                m.then_inc(s_pj, 1)

            for c in range(KC):
                x_unit(u + 1, u % 2, 0, c, LOADS)
                u += 1
            for kind, i in [v for a, b in FILL for v in a + b]:
                if kind == "x":
                    x_unit(u + 1, u % 2, 1, i, LOADS)
                else:
                    project_unit(u + 1, u % 2, kind, i, 0, KC)
                u += 1

            def units(n, k, part, first):
                base, odd = PRO_UNITS + UNITS * n, k // 4
                for kind, i in step_units(k)[part]:
                    j = unit_at(k, kind, i)
                    if kind == "x":
                        x_unit(base + j + 1, j % 2, odd, i, LOADS * (n + 2))
                    elif kind in STAT_KINDS:
                        stat_unit(kind, base + j + 1, j % 2, FZ * (n + 1) + (2 if kind == "mean" else 6))
                    else:
                        project_unit(base + j + 1, j % 2, kind, i, 1 - odd, 6 * n + 6 + 3 * odd)

            def score_blocks(out, b, p, hh, transposed, **flags):
                for hi in range(HH):
                    c, g = divmod(hh * HH + hi, 4)
                    for w in range(2):
                        cols = slice((2 * p + w) * N, (2 * p + w + 1) * N)
                        q_, k_ = qst[0:96, b, g, c, cols], kst[0:96, b, g, c, cols]
                        a, r = (k_, q_) if transposed else (q_, k_)
                        m = mm(out[w * PAD:w * PAD + N, hh, hi * N:(hi + 1) * N], a, r, **flags)
                return m

            def scores(t, n, k):
                odd, p = k // 4, k % 4
                if p == 0:
                    pe.wait_ge(s_stack[odd], STACK * (n + 1))
                need(pe, s_lg, t)
                for hh in range(2):
                    m = score_blocks(ps_sa, odd, p, hh, False, start=True, stop=True)
                m.then_inc(s_sa, 1)

            def transposed_scores(t, n, k):
                odd, p = k // 4, k % 4
                pe.wait_ge(s_dm, t + 1)
                need(pe, s_ph, t)
                kind = bias_kind(n, odd, p)
                for hh in range(2):
                    out = ps_st[:, hh, 0:HH * N]
                    mm(out, bt[0:BIAS_K, kind, :], rb[0:BIAS_K, :, :].rearrange("p h n -> p (h n)"),
                       start=True, stop=False, skip_group_check=True)
                    for part in range(2):
                        h0 = part * HEADS + hh * HH
                        mm(out, blk[:, :], dm[:, k % 2, h0:h0 + HH, :].rearrange("p h n -> p (h n)"),
                           start=False, stop=False, skip_group_check=True)
                    m = score_blocks(ps_st, odd, p, hh, True, start=False, stop=True, skip_group_check=True)
                m.then_inc(s_st, 1)

            def attend(t, n, k):
                odd, p = k // 4, k % 4
                pe.wait_ge(s_pl, t + 1)
                pe.wait_ge(s_pjr, v_unit(n, odd, p) + 1)
                need(pe, s_av, t)
                for h in range(HEADS):
                    mm(pv_out[:, h, :], ph[:, h, :], vh[:, odd, p, h, :], start=True, stop=False, skip_group_check=True)
                    mm(pv_out[:, h, 0:HD], ph[:, h, :], vl[:, odd, p, h, :], start=False, stop=False, skip_group_check=True)
                    m = mm(pv_out[:, h, :], pl[:, h, :], vh[:, odd, p, h, :], start=False, stop=True, skip_group_check=True)
                m.then_inc(s_pv, 1)

            def transpose_attended(t, k):
                pe.wait_ge(s_av, t + 1)
                need(pe, s_fin, t)
                for c in range(KC):
                    m = nc.tensor.transpose(at_out[:, c, :],
                                            av[:, 4 * c:4 * c + 4, :].rearrange("p h d -> p (h d)"),
                                            perm_out[:, 1 if k % 4 == PAIRS - 1 else 0, :])
                m.then_inc(s_at, 1)

            def project_out(t):
                pe.wait_ge(s_al, t + 1)
                for c in range(KC):
                    for n_, (a, w) in enumerate(((ath, woh), (ath, wol), (atl, woh))):
                        m = mm(ps_post[0:PT, 0:C], a[:, c, :], w[:, c, :], start=c == 0 and n_ == 0,
                               stop=c == KC - 1 and n_ == 2)
                m.then_inc(s_out, 1)

            def back(n, k, lag):
                return (n, k - lag) if k >= lag else (n - 1, k - lag + 8)

            def step(n, first=False, last=False):
                for k in range(8):
                    t = 8 * n + k
                    scores(t, n, k)
                    if not (first and k < 3):
                        transpose_attended(t - 3, k - 3 + 8)
                    if not (last and k >= 4):
                        units(n, k, 0, first)
                    if not (first and k < 2):
                        attend(t - 2, *back(n, k, 2))
                    if not (first and k < 1):
                        transposed_scores(t - 1, *back(n, k, 1))
                    if not (first and k < 3):
                        project_out(t - 3)
                    if not (last and (k >= 4 or k == 3)):
                        units(n, k, 1, first)

            pe.wait_ge(s_init, 8)
            pe.wait_ge(s_zero, 1)
            pe.wait_ge(s_bias, 6)
            step(0, first=True)
            with nc.tensor.Fori(1, LAST) as n:
                step(n)
            step(LAST, last=True)
            end = 8 * (LAST + 1)
            transpose_attended(end - 3, 5)
            attend(end - 2, LAST, 6)
            transposed_scores(end - 1, LAST, 7)
            project_out(end - 3)
            transpose_attended(end - 2, 6)
            attend(end - 1, LAST, 7)
            project_out(end - 2)
            transpose_attended(end - 1, 7)
            project_out(end - 1)


def kernel(x, L0_conv_w_qkv, L0_conv_pos_emb, L0_conv_w_out, L0_conv_b_out):
    import concourse.bacc as bacc
    from concourse.bass_utils import run_bass_kernel_spmd

    arrays = {"x": x, "w_qkv": L0_conv_w_qkv, "pos": L0_conv_pos_emb, "w_out": L0_conv_w_out,
              "b_out": L0_conv_b_out, "tables": constants()}
    arrays = {f"in_{k}": np.ascontiguousarray(v) for k, v in arrays.items()}
    nc = bacc.Bacc("TRN2", target_bir_lowering=False, num_devices=1)
    args = [nc.dram_tensor(k, a.shape, mybir.dt.from_np(a.dtype), kind="ExternalInput").ap() for k, a in arrays.items()]
    out = nc.dram_tensor("out", (B, H, W, C), mybir.dt.float32, kind="ExternalOutput").ap()
    build(nc, *args, out)
    r = run_bass_kernel_spmd(nc, [arrays], core_ids=[0])
    return r.results[0]["out"]
```

```python
from contextlib import ExitStack

import numpy as np

import concourse.bass as bass
from concourse import mybir

B, H, W, C = 16, 56, 56, 384
WS, HEADS, HD = 7, 12, 32
DISP = WS // 2
N = WS * WS
NW = W // WS
ROWS = B * (H // WS)
PAIRS = NW // 2
PT = 2 * N
RT = NW * N
PAD = 64
KC = C // 128
GROUPS = 32
GC = C // GROUPS
EPS = 1e-5
HH = HEADS // 2
TALL = WS - DISP
BIG = 1e30

SP_, SLABS, ST = 112, 4, 7
HALVES = 2 * SLABS
IMG_ROWS = H // WS
LAST = ROWS // 2 - 1

CONSTS = [("ident", 128), ("perm_in", 2 * PT), ("perm_out", 256), ("flip", 128), ("mask_rows", 512),
          ("pick", N), ("pick_scale", 2), ("mask", 4 * N), ("eye", N), ("same_window", 128),
          ("group", KC * GROUPS), ("mean_of", 128), ("ones", 128)]
CONST_AT, _at = {}, 0
for _name, _n in CONSTS:
    CONST_AT[_name] = (_at, _at + _n)
    _at += _n
CONST_COLS = _at
BIAS_K = 64 + N + 5


def place(kind, r, wc):
    if kind == 0:
        return r * 2 * WS + wc
    return wc * TALL + r if r < TALL else 2 * WS * TALL + wc * DISP + (r - TALL)


def constants():
    t = {n: np.zeros((128, k), np.float32) for n, k in CONSTS}
    t["ident"][:] = np.eye(128)
    pin = t["perm_in"].reshape(128, 2, PT)
    pout = t["perm_out"].reshape(128, 2, 128)
    for kind in range(2):
        for r in range(WS):
            for wc in range(2 * WS):
                w, c = divmod(wc, WS)
                pin[place(kind, r, wc), kind, w * N + r * WS + c] = 1
                pout[w * PAD + r * WS + c, kind, place(kind, r, wc)] = 1
        pads = [w * PAD + i for w in range(2) for i in range(N, PAD)]
        for n, p in enumerate(pads):
            pout[p, kind, PT + n] = 1
    tok = np.arange(N)
    low, right = tok // WS >= TALL, tok % WS >= TALL
    for w in range(2):
        t["flip"][N - 1 - tok, w * PAD + tok] = 1
        t["eye"][w * PAD + tok, tok] = 1
    t["pick"][N - 1 - tok, tok] = 1
    t["pick"][64 + N - 1 - tok, tok] = 1
    m0 = 64 + N
    t["pick"][m0] = BIG
    t["pick"][m0 + 1], t["pick"][m0 + 2] = BIG * right, BIG * ~right
    t["pick"][m0 + 3], t["pick"][m0 + 4] = BIG * low, BIG * ~low
    t["pick_scale"][:m0, 0] = 1
    t["pick_scale"][m0:, 1] = 1
    rows = t["mask_rows"].reshape(128, 4, 2, PAD)
    mask = t["mask"].reshape(2, PAD, 4, N)
    for bottom in range(2):
        for edge in range(2):
            kind = 2 * bottom + edge
            rows[m0, kind, :, N:] = -1
            if edge:
                rows[m0 + 1, kind, 1, :N] = -1.0 * ~right
                rows[m0 + 2, kind, 1, :N] = -1.0 * right
                mask[1, :N, kind] -= BIG * (right[:, None] != right[None, :])
            if bottom:
                rows[m0 + 3, kind, :, :N] = -1.0 * ~low
                rows[m0 + 4, kind, :, :N] = -1.0 * low
                mask[:, :N, kind] -= BIG * (low[:, None] != low[None, :])
    half = np.arange(128) // PAD
    t["same_window"][:] = -1.0 * (half[:, None] == half[None, :])
    ch = np.arange(C).reshape(KC, 128).T
    t["group"][:] = (ch[:, :, None] // GC == np.arange(GROUPS)).reshape(128, -1)
    t["mean_of"][:] = 1.0 / (SP_ * HALVES)
    t["ones"][:] = 1.0
    return np.concatenate([t[n] for n, _ in CONSTS], axis=1)


def need(eng, sem, value):
    if isinstance(value, int) and value <= 0:
        return
    eng.wait_ge(sem, value)


FILL = [([("q", 0)], [("k", 0)], [("q", 1)]),
        ([("k", 1)], [("q", 2)], [("k", 2)]),
        ([("v", 0)], [("x", 0), ("v", 1)], [("x", 1)]),
        ([("v", 2)], [("x", 2)], [("v", 3)])]
ROW_UNITS = [u for parts in FILL for part in parts for u in part]
STAT = {5: ("mean", 0), 6: ("var", 0)}
STAT_KINDS = ("mean", "var")
FZ_MEAN, FZ_SPREAD, FZ = 6, 8, 21
ROOT_STEPS = FZ - FZ_SPREAD - 1
BS_MADE, SC_MADE = 13, 18
BN_AT = [7, 7, 6, 6, 6, 0, 0, 0]


def step_units(k):
    first, second, third = FILL[k % 4]
    return first, second, third + ([STAT[k]] if k in STAT else [])


def all_units(ks):
    return [u for k in ks for part in step_units(k) for u in part]


UNITS = len(all_units(range(8)))
PRO_UNITS = 12 + 2 + 2 + 3 + 13


def unit_at(k, kind, i):
    return len(all_units(range(k))) + all_units([k]).index((kind, i))


def x_work(k, before):
    if before:
        return [(k - 1, u, c) for u, c in step_units(k - 1)[2] if u == "x"] if k else []
    return [(k, u, c) for part in step_units(k)[:2] for u, c in part if u == "x"]


assert not any(u == "x" for u, _ in step_units(7)[2])
X_TICK = [next(k for k in range(4) if ("x", c) in all_units([k])) for c in range(KC)]


ROW_FIRST = PRO_UNITS - 13


def v_unit(n, odd, p):
    if isinstance(n, int) and n == 0 and odd == 0:
        return ROW_FIRST + ROW_UNITS.index(("v", p))
    k = (0 if odd else 4) + (2 if p < 2 else 3)
    return PRO_UNITS + UNITS * (n if odd else n - 1) + unit_at(k, "v", p)


def build(nc, x, w_qkv, pos, w_out, b_out, const, y):
    fp32, f16, bf16, i32 = mybir.dt.float32, mybir.dt.float16, mybir.dt.bfloat16, mybir.dt.int32
    ALU, ACT, AX = mybir.AluOpType, mybir.ActivationFunctionType, mybir.AxisListType
    RMAX = bass.bass_isa.ReduceOp.max

    xt = x.rearrange("b h (e s) c -> b (h e) s c", s=SLABS * ST)

    ctx = ExitStack()
    with ctx:
        def sb(name, shape, dt):
            return ctx.enter_context(nc.sbuf_tensor(name, shape, dt))

        def sem(name):
            return ctx.enter_context(nc.semaphore(name))

        cst = sb("cst", [128, CONST_COLS], fp32)

        def const_of(name, rows=128):
            a, b = CONST_AT[name]
            return cst[0:rows, a:b]

        ident = const_of("ident")
        perm_in = const_of("perm_in", PT).rearrange("p (k n) -> p k n", k=2)
        perm_out = const_of("perm_out").rearrange("p (k n) -> p k n", k=2)
        mask_c = const_of("mask").rearrange("p (k n) -> p k n", k=4)
        group = const_of("group").rearrange("p (c g) -> p c g", c=KC)

        wnat = sb("wnat", [128, 9, C], fp32)
        wonat = sb("wonat", [128, 3, C], fp32)
        wh = sb("wh", [128, KC, 3 * C], f16)
        wl = sb("wl", [128, KC, 3 * C], f16)
        woh = sb("woh", [128, KC, C], f16)
        wol = sb("wol", [128, KC, C], f16)
        brow = sb("brow", [1, C], fp32)
        bout = sb("bout", [PT, C], fp32)
        amax = sb("amax", [128, 3], fp32)
        gmax = sb("gmax", [128, 3], fp32)
        p2 = sb("p2", [128, 3], fp32)
        sg = sb("sg", [128, 3], fp32)
        sc = sb("sc", [128, 8], fp32)
        bn = sb("bn", [128, N], fp32)
        bs = sb("bs", [128, N], fp32)
        bd = sb("bd", [128, N], fp32)
        bhi = sb("bhi", [128, N], f16)
        blo = sb("blo", [128, N], f16)
        bt = sb("bt", [128, 4, 128], f16)
        rb = sb("rb", [128, HH, N], bf16)
        rscale = sb("rscale", [128, 1], fp32)
        bc = sb("bc", [128, 4, N], fp32)
        blk = sb("blk", [128, 128], bf16)
        sx = sb("sx", [SP_, ST, C], fp32)
        st6 = sb("st6", [SP_, SLABS, GROUPS, 6], fp32)
        red1 = sb("red1", [SP_, GROUPS], fp32)
        red2 = sb("red2", [SP_, GROUPS], fp32)
        red3 = sb("red3", [SP_, GROUPS], fp32)
        red4 = sb("red4", [SP_, GROUPS], fp32)
        dev = sb("dev", [SP_, SLABS, 2, GROUPS], fp32)
        dev2 = sb("dev2", [SP_, SLABS, 2, GROUPS], fp32)
        meanb = sb("meanb", [128, GROUPS], fp32)
        varb = sb("varb", [128, GROUPS], fp32)
        rs0 = sb("rs0", [128, GROUPS], fp32)
        rs1 = sb("rs1", [128, GROUPS], fp32)
        rs2 = sb("rs2", [128, GROUPS], fp32)
        spread = sb("spread", [128, KC, GROUPS], fp32)
        spread2 = sb("spread2", [128, KC, GROUPS], fp32)
        coef = sb("coef", [128, B + 2, 2 * KC], fp32)
        xs = sb("xs", [PT, 2, PAIRS, C], fp32)
        xb = sb("xb", [PT, 8, C], fp32)
        xn = sb("xn", [128, 2, NW, N], fp32)
        xh = sb("xh", [128, 2, KC, NW, PAD], f16)
        xl = sb("xl", [128, 2, KC, NW, PAD], f16)
        qk = sb("qk", [128, 4, KC, RT], f16)
        stack = sb("stack", [96, 2, 4, 2, KC, RT], f16)
        vh = sb("vh", [128, 2, PAIRS, HEADS, HD + 1], f16)
        vl = sb("vl", [128, 2, PAIRS, HEADS, HD], f16)
        lg = sb("lg", [128, 2, HH, N], fp32)
        mx = sb("mx", [128, 2, HEADS], fp32)
        m2 = sb("m2", [128, 2, 2, HEADS], bf16)
        dm = sb("dm", [128, 2, 2 * HEADS, N], bf16)
        pf = sb("pf", [128, HEADS, N], fp32)
        ph = sb("ph", [128, HEADS, 2 * PAD], f16)
        pl = sb("pl", [128, HEADS, 2 * PAD], f16)
        rv = sb("rv", [128, HEADS], fp32)
        av = sb("av", [128, HEADS, HD], fp32)
        ath = sb("ath", [128, KC, PT], f16)
        atl = sb("atl", [128, KC, PT], f16)

        ps_sa = ctx.enter_context(nc.psum_tensor("ps_sa", [128, 2, 512], fp32))
        ps_st = ctx.enter_context(nc.psum_tensor("ps_st", [128, 2, 512], fp32))
        ps_pv = ctx.enter_context(nc.psum_tensor("ps_pv", [128, 512], fp32))
        ps_post = ctx.enter_context(nc.psum_tensor("ps_post", [128, 512], fp32))
        ps_pj = [ctx.enter_context(nc.psum_tensor(f"ps_pj{i}", [128, 512], fp32)) for i in range(2)]
        pv_out = ps_pv[:, 0:HEADS * (HD + 1)].rearrange("p (h d) -> p h d", h=HEADS)
        at_out = ps_post[:, 0:KC * 128].rearrange("p (c n) -> p c n", c=KC)

        s_const = sem("const_loaded")
        s_init = sem("buffers_set")
        s_zero = sem("score_banks_zeroed")
        s_cast = sem("tables_cast")
        s_pre = sem("scalars_made")
        s_gmax = sem("maxima_spread")
        s_bias = sem("bias_tables_made")
        s_slab = sem("slab_loaded")
        s_bn = sem("slab_measured")
        s_fz = sem("statistics_step")
        s_reached = sem("sp_waits_met")
        s_load = [sem("row_loaded_even"), sem("row_loaded_odd")]
        s_stack = [sem("stacks_filled_even"), sem("stacks_filled_odd")]
        s_store = [sem(f"pair_stored_{i}") for i in range(8)]
        s_pj = sem("unit_in_psum")
        s_pjr = sem("unit_taken")
        s_hi = sem("high_part_written")
        s_xh = sem("x_high_written")
        s_xl = sem("x_low_written")
        s_xb = sem("residual_made")
        s_sa = sem("scores_in_psum")
        s_lg = sem("logits_made")
        s_mx = sem("maxima_made")
        s_mh = sem("maxima_high")
        s_ml = sem("maxima_low")
        s_dm = sem("shift_tables_made")
        s_st = sem("transposed_scores_in_psum")
        s_ph = sem("probabilities_high")
        s_pl = [sem("probabilities_low_first"), sem("probabilities_low_second")]
        s_pv = sem("attended_in_psum")
        s_rv = sem("sums_inverted")
        s_av = sem("attended_normalized")
        s_at = sem("attended_transposed")
        s_ah = sem("attended_high")
        s_al = sem("attended_low")
        s_out = sem("output_in_psum")
        s_fin = sem("output_made")

        K_LOW, K_HIGH, Q_HIGH, Q_LOW = range(4)
        STACK = 12 * 16
        LOADS = (2 * 3 + 4) * 16
        STORES = [32, 32, 32, 64]

        def unit_count(n, k, kind, i):
            return PRO_UNITS + UNITS * n + unit_at(k, kind, i) + 1

        def hi_index(n, k, kind, i):
            before = 10 + 20 * n + 10 * (k // 4)
            return before + [u for u in ROW_UNITS if u[0] != "x"].index((kind, i))

        def x_units(n, k, c):
            return 6 + 6 * n + 3 * (k // 4) + c

        def x_free(n, odd):
            if isinstance(n, int) and n == 0 and not odd:
                return ROW_FIRST + ROW_UNITS.index(("v", PAIRS - 1)) + 1
            return unit_count(n if odd else n - 1, 3 if odd else 7, "v", PAIRS - 1)

        def move_row(eng, dram_, tile_of, sems, pair, load, at):
            na, nb = TALL, DISP
            image, row_a, row_b = at
            dram = dram_[image]
            split = 2 * WS * na
            pieces = []
            if pair < PAIRS - 1:
                c0 = 2 * WS * pair + DISP
                pieces.append((0, split, dram[bass.ds(row_a, na), c0:c0 + 2 * WS, :]))
                pieces.append((split, PT, dram[bass.ds(row_b, nb), c0:c0 + 2 * WS, :]))
            else:
                c0, k = 2 * WS * pair + DISP, 2 * WS - DISP
                pieces.append((0, k * na, dram[bass.ds(row_a, na), c0:W, :].rearrange("r c f -> c r f")))
                pieces.append((k * na, split, dram[bass.ds(row_a, na), 0:DISP, :].rearrange("r c f -> c r f")))
                pieces.append((split, split + k * nb, dram[bass.ds(row_b, nb), c0:W, :].rearrange("r c f -> c r f")))
                pieces.append((split + k * nb, PT, dram[bass.ds(row_b, nb), 0:DISP, :].rearrange("r c f -> c r f")))
            for a, b, d in pieces:
                t = tile_of[a:b]
                if load:
                    eng.dma_start(t, d).then_inc(sems, 16)
                else:
                    eng.dma_start(d, t).then_inc(sems, 16)

        def rows_of(n, odd):
            first = 2 * WS * (n & 3) + WS * odd
            after = 2 * WS * ((n + 1) & 3) if odd else first + WS
            return (n >> 2) & (B - 1), first + DISP, after

        def bias_kind(n, odd, pair):
            edge = 1 if pair == PAIRS - 1 else 0
            if not odd:
                return edge
            return (((n & 3) + 1) >> 2) * 2 + edge

        block = ctx.enter_context(nc.Block())

        @block.sync
        def _(sp):
            sp.dma_start(cst[:, :], const[:, :]).then_inc(s_const, 16)
            sp.dma_start(wnat[:, :, :], w_qkv.rearrange("(a p) c -> p a c", p=128)).then_inc(s_const, 16)
            sp.dma_start(wonat[:, :, :], w_out.rearrange("(a p) c -> p a c", p=128)).then_inc(s_const, 16)
            sp.dma_start(brow[:, :], b_out.rearrange("(a c) -> a c", a=1)).then_inc(s_const, 16)
            def slab(img, s):
                sp.dma_start(sx[:, :, :], xt[img, :, s * ST:(s + 1) * ST, :]).then_inc(s_slab, 16)
            slab(0, 0)
            sp.wait_ge(s_init, 1)
            for r in range(WS):
                for c in range(WS):
                    for at in (0, 64):
                        q = at + r * WS + c
                        sp.dma_start(bn[q:q + 1, :].rearrange("p (r c) -> p r c", r=WS),
                                     pos[r:r + WS, c:c + WS].rearrange("(a r) c -> a r c", a=1)).then_inc(s_const, 16)
            def load_row(n, odd):
                at = rows_of(n, odd)
                for p in range(PAIRS):
                    move_row(sp, x, xs[:, odd, p, :], s_load[odd], p, True, at)
            load_row(0, 0)
            load_row(0, 1)
            for s in range(1, SLABS):
                sp.wait_ge(s_bn, s)
                slab(0, s)
            sp.wait_ge(s_bn, SLABS)
            slab(1, 0)
            sp.wait_ge(s_bn, SLABS + 1)
            slab(1, 1)

            def reach(sem, value):
                if not (isinstance(value, int) and value <= 0):
                    sp.wait_ge(sem, value)
                    sp.sem_inc(s_reached, 1)

            def stack_row(b, done_units, free):
                reach(s_pjr, done_units)
                reach(s_st, free)
                for part, (kp, qp) in enumerate(((K_HIGH, Q_HIGH), (K_HIGH, Q_LOW), (K_LOW, Q_HIGH))):
                    to = slice(32 * part, 32 * part + 32)
                    for g in range(4):
                        sp.dma_start(stack[to, b, g, :, :, :],
                                     qk[32 * g:32 * g + 32, kp:qp + 1:qp - kp, :, :]).then_inc(s_stack[b], 16)

            stack_row(0, ROW_FIRST + 6, 0)

            def step(n, first=False, last=False):
                for k in range(8):
                    odd, p, t = k // 4, k % 4, 8 * n + k
                    if p == 0 and not last:
                        reach(s_xb, 8 * n + 4 * odd + 4)
                        reach(s_pj, ROW_FIRST + 13 if first and odd else
                             (ROW_FIRST if first else unit_count(n - 1, 4 * odd + X_TICK[2], "x", 2)))
                        load_row(n + 1, odd)
                    if p == 2 and not (last and odd):
                        stack_row(1 - odd, unit_count(n, 4 * odd + 1, "k", 2), 8 * n + 4 * odd)
                    if k == 5 and not last:
                        m = n + 2
                        reach(s_bn, SLABS + 2 + n)
                        slab_at = (m & 3) * ST
                        img = ((m >> 2) + 1) & (B - 1)
                        sp.dma_start(sx[:, :, :], xt[img, :, bass.ds(slab_at, ST), :]).then_inc(s_slab, 16)
                    if not (first and k < 3):
                        store(t - 3, n, k - 3)

            def store(t, n, j):
                reach(s_fin, t + 1)
                if j < 0:
                    n, j = n - 1, j + 8
                at = rows_of(n, j // 4)
                move_row(sp, y, xb[:, j, :], s_store[j], j % 4, False, at)

            step(0, first=True)
            with nc.sync.Fori(1, LAST) as n:
                step(n)
            step(LAST, last=True)
            for j in range(5, 8):
                store(8 * LAST + j, LAST, j)
            for j in range(8):
                sp.wait_ge(s_store[j], STORES[j % 4] * (LAST + 1))

        @block.gpsimd
        def _(pool):
            nc.gpsimd.memset(bn[:, :], 0.0).then_inc(s_init, 1)
            nc.gpsimd.memset(xh[:, :, :, :, :], 0.0).then_inc(s_init, 1)
            nc.gpsimd.memset(xl[:, :, :, :, :], 0.0).then_inc(s_init, 1)
            nc.gpsimd.memset(vh[:, :, :, :, :], 1.0).then_inc(s_init, 1)
            nc.gpsimd.memset(ph[:, :, :], 0.0).then_inc(s_init, 1)
            nc.gpsimd.memset(pl[:, :, :], 0.0).then_inc(s_init, 1)
            pool.wait_ge(s_init, 5)
            for w in range(2):
                nc.gpsimd.memset(ph[:, :, w * PAD + N:(w + 1) * PAD], 1.0).then_inc(s_init, 1)
            pool.wait_ge(s_pre, 3)
            nc.gpsimd.partition_all_reduce(gmax[:, :], amax[:, :], 128, RMAX).then_inc(s_gmax, 1)

            def x_low(unit, index, slot, b, c, used):
                pool.wait_ge(s_pjr, unit)
                pool.wait_ge(s_xh, index + 1)
                need(pool, s_pj, used)
                nc.gpsimd.tensor_tensor(xl[:, b, c, :, 0:N], xn[:, slot, :, :], xh[:, b, c, :, 0:N],
                                        ALU.subtract).then_inc(s_xl, 1)

            def residual(t, n, j, first=False):
                if j >= 8:
                    n, j = n + 1, j - 8
                pool.wait_ge(s_load[j // 4], LOADS * (n + 1))
                need(pool, s_store[j], STORES[j % 4] * n)
                nc.gpsimd.tensor_tensor(xb[:, j, :], xs[:, j // 4, j % 4, :], bout[:, :], ALU.add).then_inc(s_xb, 1)

            for c in range(KC):
                x_low(ROW_FIRST - KC + c + 1, c, c % 2, 0, c, 0)
            for c in range(KC):
                x_low(ROW_FIRST + ROW_UNITS.index(("x", c)) + 1, KC + c, (KC + c) % 2, 1, c, 0)
            pool.wait_ge(s_pjr, 14)
            for j in range(3):
                residual(j, 0, j)

            def split_probabilities(t, x_lows):
                pool.wait_ge(s_dm, t + 2 if not isinstance(t, int) else min(t + 2, 8 * (LAST + 1)))
                pool.wait_ge(s_xl, x_lows)
                pool.wait_ge(s_ph, t + 1)
                need(pool, s_pv, t)
                nc.gpsimd.tensor_tensor(pl[PAD:, :, PAD:PAD + N], pf[PAD:, :, :], ph[PAD:, :, PAD:PAD + N],
                                        ALU.subtract).then_inc(s_pl[1], 1)

            def x_lows(n, k, before):
                for at, kind, c in x_work(k, before):
                    odd = at // 4
                    x_low(unit_count(n, at, kind, c), x_units(n, at, c), (odd + c) % 2, odd, c, x_free(n, odd))

            def step(n, first=False, last=False):
                for k in range(8):
                    t = 8 * n + k
                    if not (first and k < 2):
                        x_before = sum(len(x_work(i, before)) for i in range(min(k, 4) if last else k)
                                       for before in (True, False))
                        split_probabilities(t - 2, 6 + 6 * n + x_before)
                        pool.wait_ge(s_pl[1], t - 1)
                    if not (last and k >= 4):
                        x_lows(n, k, True)
                    if not (last and k + 3 >= 8):
                        residual(t + 3, n, k + 3, first)
                    pool.wait_ge(s_ml, t + 1)
                    need(pool, s_st, t - 1)
                    nc.gpsimd.tensor_tensor(
                        dm[:, k % 2, :, :],
                        const_of("eye").unsqueeze(1).broadcast_to([128, 2 * HEADS, N]),
                        m2[:, k % 2, :, :].rearrange("p a h -> p (a h)").unsqueeze(2).broadcast_to([128, 2 * HEADS, N]),
                        ALU.mult).then_inc(s_dm, 1)
                    if not (last and k >= 4):
                        x_lows(n, k, False)

            step(0, first=True)
            with nc.gpsimd.Fori(1, LAST) as n:
                step(n)
            step(LAST, last=True)
            split_probabilities(8 * (LAST + 1) - 2, 6 * LAST + 9)
            split_probabilities(8 * (LAST + 1) - 1, 6 * LAST + 9)

        @block.scalar
        def _(act):
            def high(unit, kind, i, b, p_free, stack_sem, stack_need, bank):
                act.wait_ge(s_pj, unit)
                if kind == "v":
                    need(act, s_pv, p_free)
                    nc.scalar.activation(vh[:, b, i, :, 0:HD], ps_pj[bank][:, 0:C].rearrange("p (h d) -> p h d", h=HEADS),
                                         ACT.Copy).then_inc(s_hi, 1)
                else:
                    need(act, stack_sem, stack_need)
                    nc.scalar.activation(qk[:, K_HIGH if kind == "k" else Q_HIGH, i, :], ps_pj[bank][:, 0:RT],
                                         ACT.Copy).then_inc(s_hi, 1)

            def x_high(unit, slot, b, c, used):
                act.wait_ge(s_pjr, unit)
                need(act, s_pj, used)
                nc.scalar.activation(xh[:, b, c, :, 0:N], xn[:, slot, :, :], ACT.Copy).then_inc(s_xh, 1)

            act.wait_ge(s_init, 8)
            for c in range(KC):
                x_high(ROW_FIRST - KC + c + 1, c % 2, 0, c, 0)
            u = ROW_FIRST
            for kind, i in ROW_UNITS:
                if kind == "x":
                    x_high(u + 1, (KC + i) % 2, 1, i, 0)
                else:
                    high(u + 1, kind, i, 0, 0, None, 0, u % 2)
                u += 1

            def units(n, k, parts):
                base = PRO_UNITS + UNITS * n
                odd = k // 4
                for kind, i in [u for part in parts for u in step_units(k)[part]]:
                    j = unit_at(k, kind, i)
                    if kind not in STAT_KINDS and kind != "x":
                        high(base + j + 1, kind, i, 1 - odd, 8 * n + 4 * odd - 4 + i + 1,
                             s_stack[odd], STACK * (n + 1), j % 2)

            def x_highs(n, k, before):
                for at, kind, c in x_work(k, before):
                    odd = at // 4
                    x_high(unit_count(n, at, kind, c), (odd + c) % 2, odd, c, x_free(n, odd))

            def step(n, first=False, last=False):
                for k in range(8):
                    t = 8 * n + k
                    if not (first and k < 3):
                        attended_high(t - 3)
                    if not (last and k >= 4):
                        units(n, k, (0, 1))
                        x_highs(n, k, True)
                        x_highs(n, k, False)
                    if not (first and k < 1):
                        probabilities(t - 1)
                    if not (last and k >= 4):
                        units(n, k, (2,))

            def attended_high(t):
                act.wait_ge(s_at, t + 1)
                need(act, s_out, t)
                nc.scalar.activation(ath[:, :, :], at_out[:, :, 0:PT], ACT.Copy).then_inc(s_ah, 1)

            def probabilities(t):
                act.wait_ge(s_st, t + 1)
                for w in range(2):
                    need(act, s_pl[w], t)
                nc.scalar.activation(pf[:, :, :].rearrange("p (a h) n -> p a (h n)", a=2), ps_st[:, :, 0:HH * N], ACT.Exp,
                                     scale=sc[:, 0:1])
                need(act, s_pv, t)
                for w in range(2):
                    rows = slice(w * PAD, (w + 1) * PAD)
                    e = nc.scalar.activation(
                        ph[rows, :, w * PAD:w * PAD + N].rearrange("p (a h) n -> p a h n", a=2),
                        ps_st[rows, :, 0:HH * N].rearrange("p a (h n) -> p a h n", h=HH), ACT.Exp, scale=sc[rows, 0:1])
                e.then_inc(s_ph, 1)

            act.wait_ge(s_pre, SC_MADE)
            step(0, first=True)
            with nc.scalar.Fori(1, LAST) as n:
                step(n)
            step(LAST, last=True)
            end = 8 * (LAST + 1)
            attended_high(end - 3)
            probabilities(end - 1)
            attended_high(end - 2)
            attended_high(end - 1)

        @block.vector
        def _(dve):
            made = [0]

            def pre(ins):
                made[0] += 1
                ins.then_inc(s_pre, 1)
                dve.wait_ge(s_pre, made[0])

            nc.vector.memset(ps_sa[:, :, :], 0.0).then_inc(s_zero, 1)
            dve.wait_ge(s_const, 16 * (4 + 2 * N))
            nc.vector.tensor_reduce(amax[:, 0:1], wnat[:, :, :], AX.XY, ALU.max, apply_absolute_value=True).then_inc(s_pre, 1)
            nc.vector.tensor_reduce(amax[:, 1:2], wonat[:, :, :], AX.XY, ALU.max, apply_absolute_value=True).then_inc(s_pre, 1)
            nc.vector.tensor_reduce(amax[:, 2:3], bn[:, :], AX.X, ALU.max, apply_absolute_value=True).then_inc(s_pre, 1)
            made[0] = 3
            dve.wait_ge(s_gmax, 1)
            pre(nc.vector.tensor_scalar(gmax[:, 0:2], gmax[:, 0:2], 2.0 ** -20, None, ALU.max))
            pre(nc.vector.tensor_scalar(p2[:, 0:2].bitcast(i32), gmax[:, 0:2].bitcast(i32), 0x7F800000, None, ALU.bitwise_and))
            pre(nc.vector.reciprocal(sg[:, 0:2], p2[:, 0:2]))
            pre(nc.vector.scalar_tensor_tensor(sc[:, 0:1], p2[:, 0:1], HD ** -0.5, p2[:, 0:1], ALU.mult, ALU.mult))
            pre(nc.vector.scalar_tensor_tensor(sc[:, 1:2], sg[:, 0:1], HD ** 0.5, sg[:, 0:1], ALU.mult, ALU.mult))
            pre(nc.vector.tensor_tensor(sc[:, 2:3], p2[:, 0:1], p2[:, 1:2], ALU.mult))
            pre(nc.vector.tensor_scalar(gmax[:, 2:3], gmax[:, 2:3], sc[:, 1:2], 2.0 ** -60, ALU.mult, ALU.max))
            pre(nc.vector.tensor_scalar(p2[:, 2:3].bitcast(i32), gmax[:, 2:3].bitcast(i32), 0x7F800000, None, ALU.bitwise_and))
            pre(nc.vector.reciprocal(sg[:, 2:3], p2[:, 2:3]))
            pre(nc.vector.tensor_scalar(bs[:, :], bn[:, :], sc[:, 1:2], None, ALU.mult))
            assert made[0] == BS_MADE
            pre(nc.vector.tensor_scalar(bd[:, :], bs[:, :], sg[:, 2:3], None, ALU.mult))
            pre(nc.vector.tensor_copy(bhi[:, :], bd[:, :]))
            pre(nc.vector.tensor_tensor(blo[:, :], bd[:, :], bhi[:, :], ALU.subtract))
            pre(nc.vector.tensor_copy(bt[:, :, :].rearrange("p a b -> p (a b)"), const_of("mask_rows")))
            for w in range(2):
                cols = slice(w * PAD, w * PAD + N)
                for part, at in ((bhi, 0), (blo, 64)):
                    nc.vector.tensor_copy(bt[at:at + N, :, cols],
                                          part[at:at + N, :].unsqueeze(1).broadcast_to([N, 4, N])).then_inc(s_bias, 1)
            ps_ = const_of("pick_scale")
            pre(nc.vector.scalar_tensor_tensor(rscale[:, :], ps_[:, 0:1], p2[:, 2:3], ps_[:, 1:2], ALU.mult, ALU.add))
            nc.vector.tensor_scalar(rb[:, :, :], const_of("pick").unsqueeze(1).broadcast_to([128, HH, N]),
                                    rscale[:, 0:1], None, ALU.mult).then_inc(s_bias, 1)
            nc.vector.tensor_copy(blk[:, :], const_of("same_window")).then_inc(s_bias, 1)
            assert made[0] == SC_MADE

            u = 0
            for kind in ("w", "o"):
                for c in range(KC):
                    for a in range(3 if kind == "w" else 1):
                        hi_, lo_ = (wh, wl) if kind == "w" else (woh, wol)
                        s = sg[:, 0:1] if kind == "w" else sg[:, 1:2]
                        cols = slice(a * C, (a + 1) * C)
                        dve.wait_ge(s_pj, u + 1)
                        nc.vector.tensor_scalar(hi_[:, c, cols], ps_pj[u % 2][:, 0:C], s, None, ALU.mult).then_inc(s_cast, 1)
                        dve.wait_ge(s_cast, u + 1)
                        nc.vector.scalar_tensor_tensor(lo_[:, c, cols], ps_pj[u % 2][:, 0:C], s, hi_[:, c, cols],
                                                       ALU.mult, ALU.subtract).then_inc(s_pjr, 1)
                        u += 1
            dve.wait_ge(s_pj, u + 1)
            nc.vector.tensor_tensor(bc[:, :, :], mask_c, ps_pj[u % 2][:, 0:N].unsqueeze(1).broadcast_to([128, 4, N]),
                                    ALU.add).then_inc(s_pjr, 1)
            u += 1
            dve.wait_ge(s_pj, u + 1)
            nc.vector.tensor_copy(bout[:, :], ps_pj[u % 2][0:PT, 0:C]).then_inc(s_pjr, 1)
            u += 1

            def measure(slab_slot, groups, done):
                for g in groups:
                    last = nc.vector.bn_stats(st6[:, slab_slot, g, :], sx[:, :, g * GC:(g + 1) * GC])
                if done:
                    last.then_inc(s_bn, 1)

            def stat_sums():
                nc.vector.tensor_reduce(red1[:, :], st6[:, :, :, 1:5:3].rearrange("p s g e -> p g s e"), AX.XY,
                                        ALU.add).then_inc(s_fz, 1)
                nc.vector.tensor_reduce(red2[:, :], st6[:, :, :, 2:6:3].rearrange("p s g e -> p g s e"), AX.XY,
                                        ALU.add).then_inc(s_fz, 1)

            def stat_mean(unit, bank, base):
                dve.wait_ge(s_pj, unit)
                nc.vector.tensor_copy(meanb[:, :], ps_pj[bank][:, 0:GROUPS]).then_inc(s_pjr, 1)
                dve.wait_ge(s_pjr, unit)
                nc.vector.tensor_tensor(dev[:, :, :, :], st6[:, :, :, 1:5:3].rearrange("p s g e -> p s e g"),
                                        meanb[0:SP_, :].unsqueeze(1).unsqueeze(1).broadcast_to([SP_, SLABS, 2, GROUPS]),
                                        ALU.subtract).then_inc(s_fz, 1)
                dve.wait_ge(s_fz, base + 3)
                nc.vector.tensor_tensor(dev2[:, :, :, :], dev[:, :, :, :], dev[:, :, :, :], ALU.mult).then_inc(s_fz, 1)
                dve.wait_ge(s_fz, base + 4)
                nc.vector.tensor_reduce(red3[:, :], dev2[:, :, :, :].rearrange("p s e g -> p g (s e)"), AX.X,
                                        ALU.add).then_inc(s_fz, 1)
                dve.wait_ge(s_fz, base + 5)
                nc.vector.scalar_tensor_tensor(red4[:, :], red2[:, :], 2.0 / (ST * GC), red3[:, :], ALU.mult,
                                               ALU.add).then_inc(s_fz, 1)

            def stat_spread_mean(slot, base, i):
                dve.wait_ge(s_fz, base + FZ_MEAN + i)
                if i == 0:
                    ins = nc.vector.tensor_tensor(spread[:, :, :], group, meanb[:, :].unsqueeze(1).broadcast_to(
                        [128, KC, GROUPS]), ALU.mult)
                else:
                    ins = nc.vector.tensor_reduce(coef[:, slot, 0:KC], spread[:, :, :], AX.X, ALU.add)
                ins.then_inc(s_fz, 1)

            def stat_var(unit, bank):
                dve.wait_ge(s_pj, unit)
                nc.vector.tensor_scalar(varb[:, :], ps_pj[bank][:, 0:GROUPS], EPS, None, ALU.add).then_inc(s_pjr, 1)
                dve.wait_ge(s_pjr, unit)
                nc.vector.tensor_scalar(rs1[:, :].bitcast(i32), varb[:, :].bitcast(i32), 1, None,
                                        ALU.logical_shift_right).then_inc(s_fz, 1)

            def stat_root(slot, base, i):
                v, y = varb[:, :], rs0[:, :]
                dve.wait_ge(s_fz, base + FZ_SPREAD + 1 + i)
                if i == 0:
                    ins = nc.vector.tensor_scalar(y.bitcast(i32), rs1[:, :].bitcast(i32), -1.0, float(0x5F3759DF),
                                                  ALU.mult, ALU.add)
                elif i < 10 and i % 3 == 1:
                    ins = nc.vector.scalar_tensor_tensor(rs1[:, :], y, -0.5, v, ALU.mult, ALU.mult)
                elif i < 10 and i % 3 == 2:
                    ins = nc.vector.tensor_tensor(rs2[:, :], rs1[:, :], y, ALU.mult)
                elif i < 10:
                    ins = nc.vector.scalar_tensor_tensor(y, rs2[:, :], 1.5, y, ALU.add, ALU.mult)
                elif i == 10:
                    ins = nc.vector.tensor_tensor(spread2[:, :, :], group, y.unsqueeze(1).broadcast_to(
                        [128, KC, GROUPS]), ALU.mult)
                else:
                    ins = nc.vector.tensor_reduce(coef[:, slot, KC:2 * KC], spread2[:, :, :], AX.X, ALU.add)
                ins.then_inc(s_fz, 1)

            for s in range(SLABS):
                dve.wait_ge(s_slab, 16 * (s + 1))
                measure(s, range(GROUPS), True)
            dve.wait_ge(s_bn, SLABS)
            stat_sums()
            stat_mean(u + 1, u % 2, 0)
            for i in range(2):
                stat_spread_mean(0, 0, i)
            stat_var(u + 2, (u + 1) % 2)
            for i in range(ROOT_STEPS):
                stat_root(0, 0, i)
            u += 2
            dve.wait_ge(s_slab, 16 * (SLABS + 1))
            measure(0, range(GROUPS), True)
            dve.wait_ge(s_fz, FZ)

            def x_norm(unit, bank, index, slot, img, c):
                dve.wait_ge(s_pj, unit)
                need(dve, s_xh, index - 1)
                need(dve, s_xl, index - 1)
                nc.vector.tensor_scalar(xn[:, slot, :, :].rearrange("p w n -> p (w n)"), ps_pj[bank][:, 0:RT],
                                        coef[:, img, c:c + 1], coef[:, img, KC + c:KC + c + 1],
                                        ALU.subtract, ALU.mult).then_inc(s_pjr, 1)

            def low(bank, hi, kind, i, b, p_free, stack_sem, stack_need):
                dve.wait_ge(s_hi, hi)
                if kind == "v":
                    need(dve, s_pv, p_free)
                    nc.vector.tensor_tensor(vl[:, b, i, :, :], ps_pj[bank][:, 0:C].rearrange("p (h d) -> p h d", h=HEADS),
                                            vh[:, b, i, :, 0:HD], ALU.subtract).then_inc(s_pjr, 1)
                else:
                    need(dve, stack_sem, stack_need)
                    hp, lp = (K_HIGH, K_LOW) if kind == "k" else (Q_HIGH, Q_LOW)
                    nc.vector.tensor_tensor(qk[:, lp, i, :], ps_pj[bank][:, 0:RT], qk[:, hp, i, :],
                                            ALU.subtract).then_inc(s_pjr, 1)

            for c in range(KC):
                x_norm(u + 1, u % 2, c, c % 2, 0, c)
                u += 1
            h = 0
            for kind, i in ROW_UNITS:
                if kind == "x":
                    x_norm(u + 1, u % 2, KC + i, (KC + i) % 2, 0, i)
                else:
                    low(u % 2, h + 1, kind, i, 0, 0, None, 0)
                    h += 1
                u += 1
            assert u == PRO_UNITS

            def units(n, k, part, first):
                base, odd = PRO_UNITS + UNITS * n, k // 4
                for kind, i in step_units(k)[part]:
                    j = unit_at(k, kind, i)
                    if kind == "x":
                        if i == 0:
                            dve.wait_ge(s_fz, FZ * (n + 1))
                        x_norm(base + j + 1, j % 2, x_units(n, k, i), (odd + i) % 2, (n + 1) >> 2, i)
                    elif kind == "mean":
                        stat_mean(base + j + 1, j % 2, FZ * (n + 1))
                    elif kind == "var":
                        stat_var(base + j + 1, j % 2)
                    else:
                        low(j % 2, hi_index(n, k, kind, i) + 1, kind, i, 1 - odd,
                            8 * n + 4 * odd - 4 + i + 1, s_stack[odd], STACK * (n + 1))

            def logits(t, n, k):
                dve.wait_ge(s_sa, t + 1)
                bias = bc[:, bias_kind(n, k // 4, k % 4), :]
                nc.vector.tensor_tensor(lg[:, :, :, :], ps_sa[:, :, 0:HH * N].rearrange("p a (h n) -> p a h n", h=HH),
                                        bias.unsqueeze(1).unsqueeze(1).broadcast_to([128, 2, HH, N]),
                                        ALU.add).then_inc(s_lg, 1)

            def attended_low(t):
                dve.wait_ge(s_ah, t + 1)
                need(dve, s_out, t)
                nc.vector.tensor_tensor(atl[:, :, :], at_out[:, :, 0:PT], ath[:, :, :], ALU.subtract).then_inc(s_al, 1)

            def maxima(t, k):
                dve.wait_ge(s_lg, t + 1)
                nc.vector.tensor_reduce(mx[:, k % 2, :], lg[:, :, :, :].rearrange("p a h n -> p (a h) n"), AX.X,
                                        ALU.max).then_inc(s_mx, 1)

            def maxima_high(t, k):
                dve.wait_ge(s_mx, t + 1)
                need(dve, s_dm, t - 1)
                nc.vector.tensor_copy(m2[:, k % 2, 0, :], mx[:, k % 2, :]).then_inc(s_mh, 1)

            def maxima_low(t, k):
                dve.wait_ge(s_mh, t + 1)
                nc.vector.tensor_tensor(m2[:, k % 2, 1, :], mx[:, k % 2, :], m2[:, k % 2, 0, :], ALU.subtract).then_inc(s_ml, 1)

            def invert(t):
                dve.wait_ge(s_pv, t + 1)
                nc.vector.reciprocal(rv[:, :], pv_out[:, :, HD]).then_inc(s_rv, 1)

            def normalize(t):
                dve.wait_ge(s_rv, t + 1)
                need(dve, s_at, t)
                nc.vector.tensor_tensor(av[:, :, :], pv_out[:, :, 0:HD], rv[:, :].unsqueeze(2).broadcast_to([128, HEADS, HD]),
                                        ALU.mult).then_inc(s_av, 1)

            def output(t, j):
                dve.wait_ge(s_out, t + 1)
                dve.wait_ge(s_xb, t + 1)
                nc.vector.scalar_tensor_tensor(xb[:, j % 8, :], ps_post[0:PT, 0:C], sc[0:PT, 2:3], xb[:, j % 8, :],
                                               ALU.mult, ALU.add).then_inc(s_fin, 1)

            def split_probabilities(t):
                dve.wait_ge(s_ph, t + 1)
                need(dve, s_pv, t)
                nc.vector.tensor_tensor(pl[0:PAD, :, 0:N], pf[0:PAD, :, :], ph[0:PAD, :, 0:N],
                                        ALU.subtract).then_inc(s_pl[0], 1)

            def step(n, first=False, last=False):
                measured = 0
                steps = iter(range(ROOT_STEPS) if not last else ())

                def between():
                    i = next(steps, None) if k == 7 else None
                    if i is not None:
                        stat_root(((n + 1) >> 2) + 1, FZ * (n + 1), i)

                for k in range(8):
                    t = 8 * n + k
                    between()
                    logits(t, n, k)
                    between()
                    if not (first and k < 3):
                        attended_low(t - 3)
                    between()
                    maxima(t, k)
                    between()
                    maxima_high(t, k)
                    between()
                    if not (last and k >= 4):
                        units(n, k, 0, first)
                    between()
                    maxima_low(t, k)
                    if not (first and k < 2):
                        invert(t - 2)
                    between()
                    if not (first and k < 2):
                        normalize(t - 2)
                    between()
                    if not (last and k >= 4):
                        units(n, k, 1, first)
                    if not last and k == 0:
                        dve.wait_ge(s_slab, 16 * (SLABS + 2 + n))
                    if not last and BN_AT[k]:
                        measure((n + 1) & 3, range(measured, measured + BN_AT[k]), measured + BN_AT[k] == GROUPS)
                        measured += BN_AT[k]
                    if not last and k == 5:
                        dve.wait_ge(s_bn, SLABS + 2 + n)
                        stat_sums()
                    if not last and k == 6:
                        for i in range(2):
                            stat_spread_mean(((n + 1) >> 2) + 1, FZ * (n + 1), i)
                    between()
                    if not (first and k < 3):
                        output(t - 3, k - 3)
                    between()
                    if not (first and k < 1):
                        split_probabilities(t - 1)
                    between()
                    if not (last and k >= 4):
                        units(n, k, 2, first)
                    between()

            step(0, first=True)
            with nc.vector.Fori(1, LAST) as n:
                step(n)
            step(LAST, last=True)
            end = 8 * (LAST + 1)
            attended_low(end - 3)
            invert(end - 2)
            normalize(end - 2)
            output(end - 3, 5)
            split_probabilities(end - 1)
            attended_low(end - 2)
            invert(end - 1)
            normalize(end - 1)
            output(end - 2, 6)
            attended_low(end - 1)
            output(end - 1, 7)

        @block.tensor
        def _(pe):
            mm = nc.tensor.matmul

            def bank_free(unit):
                need(pe, s_pjr, unit - 2)

            pe.wait_ge(s_const, 16 * (4 + 2 * N))
            u = 0
            for kind in ("w", "o"):
                for c in range(KC):
                    for a in range(3 if kind == "w" else 1):
                        bank_free(u + 1)
                        for i in range(3):
                            src = wnat[:, 3 * a + i, :] if kind == "w" else wonat[:, i, :]
                            m = nc.tensor.transpose(ps_pj[u % 2][:, i * 128:(i + 1) * 128], src[:, c * 128:(c + 1) * 128], ident)
                        m.then_inc(s_pj, 1)
                        u += 1
            bank_free(u + 1)
            pe.wait_ge(s_pre, BS_MADE)
            mm(ps_pj[u % 2][:, 0:N], const_of("flip", N), bs[0:N, :], start=True, stop=True).then_inc(s_pj, 1)
            u += 1
            bank_free(u + 1)
            mm(ps_pj[u % 2][0:PT, 0:C], const_of("ones", 1)[:, 0:PT], brow[:, :], start=True, stop=True).then_inc(s_pj, 1)
            u += 1

            def stat_unit(kind, unit, bank, fz):
                bank_free(unit)
                pe.wait_ge(s_fz, fz)
                mm(ps_pj[bank][:, 0:GROUPS], const_of("mean_of", SP_), (red1 if kind == "mean" else red4)[:, :],
                   start=True, stop=True).then_inc(s_pj, 1)

            stat_unit("mean", u + 1, u % 2, 2)
            stat_unit("var", u + 2, (u + 1) % 2, FZ_MEAN)
            u += 2

            def x_unit(unit, bank, b, c, loaded):
                bank_free(unit)
                pe.wait_ge(s_load[b], loaded)
                for p in range(PAIRS):
                    m = nc.tensor.transpose(ps_pj[bank][:, p * PT:(p + 1) * PT], xs[:, b, p, c * 128:(c + 1) * 128],
                                            perm_in[:, 1 if p == PAIRS - 1 else 0, :])
                m.then_inc(s_pj, 1)

            def project_unit(unit, bank, kind, i, b, x_ready):
                bank_free(unit)
                pe.wait_ge(s_xh, x_ready)
                pe.wait_ge(s_xl, x_ready)
                for c in range(KC):
                    for n_, (xa, wa) in enumerate(((xh, wh), (xh, wl), (xl, wh))):
                        on = dict(start=c == 0 and n_ == 0, stop=c == KC - 1 and n_ == 2)
                        if kind == "v":
                            m = mm(ps_pj[bank][:, 0:C], xa[:, b, c, 2 * i:2 * i + 2, :].rearrange("p w n -> p (w n)"),
                                   wa[:, c, 2 * C:3 * C], **on)
                        else:
                            o = (C if kind == "k" else 0) + i * 128
                            m = mm(ps_pj[bank][:, 0:RT].rearrange("p (w n) -> p w n", w=NW), wa[:, c, o:o + 128],
                                   xa[:, b, c, :, 0:N], **on)
                m.then_inc(s_pj, 1)

            for c in range(KC):
                x_unit(u + 1, u % 2, 0, c, LOADS)
                u += 1
            for kind, i in ROW_UNITS:
                if kind == "x":
                    x_unit(u + 1, u % 2, 1, i, LOADS)
                else:
                    project_unit(u + 1, u % 2, kind, i, 0, KC)
                u += 1

            def units(n, k, part, last):
                base, odd = PRO_UNITS + UNITS * n, k // 4
                for kind, i in step_units(k)[part]:
                    j = unit_at(k, kind, i)
                    if kind == "x":
                        x_unit(base + j + 1, j % 2, odd, i, LOADS * (n + (1 if last else 2)))
                    elif kind in STAT_KINDS:
                        stat_unit(kind, base + j + 1, j % 2, FZ * (n + 1) + (2 if kind == "mean" else FZ_MEAN))
                    else:
                        project_unit(base + j + 1, j % 2, kind, i, 1 - odd, 6 * n + 6 + 3 * odd)

            def score_blocks(out, b, p, hh, transposed, **flags):
                for hi in range(HH):
                    c, g = divmod(hh * HH + hi, 4)
                    for w in range(2):
                        cols = slice((2 * p + w) * N, (2 * p + w + 1) * N)
                        k_, q_ = stack[0:96, b, g, 0, c, cols], stack[0:96, b, g, 1, c, cols]
                        a, r = (k_, q_) if transposed else (q_, k_)
                        m = mm(out[w * PAD:w * PAD + N, hh, hi * N:(hi + 1) * N], a, r, **flags)
                return m

            def scores(t, n, k):
                odd, p = k // 4, k % 4
                if p == 0:
                    pe.wait_ge(s_stack[odd], STACK * (n + 1))
                need(pe, s_lg, t)
                for hh in range(2):
                    m = score_blocks(ps_sa, odd, p, hh, False, start=True, stop=True)
                m.then_inc(s_sa, 1)

            def transposed_scores(t, n, k):
                odd, p = k // 4, k % 4
                pe.wait_ge(s_dm, t + 1)
                need(pe, s_ph, t)
                kind = bias_kind(n, odd, p)
                for hh in range(2):
                    out = ps_st[:, hh, 0:HH * N]
                    mm(out, bt[0:BIAS_K, kind, :], rb[0:BIAS_K, :, :].rearrange("p h n -> p (h n)"),
                       start=True, stop=False, skip_group_check=True)
                    for part in range(2):
                        h0 = part * HEADS + hh * HH
                        mm(out, blk[:, :], dm[:, k % 2, h0:h0 + HH, :].rearrange("p h n -> p (h n)"),
                           start=False, stop=False, skip_group_check=True)
                    m = score_blocks(ps_st, odd, p, hh, True, start=False, stop=True, skip_group_check=True)
                m.then_inc(s_st, 1)

            def attend(t, n, k):
                odd, p = k // 4, k % 4
                for w in range(2):
                    pe.wait_ge(s_pl[w], t + 1)
                pe.wait_ge(s_pjr, v_unit(n, odd, p) + 1)
                need(pe, s_av, t)
                for h in range(HEADS):
                    mm(pv_out[:, h, :], ph[:, h, :], vh[:, odd, p, h, :], start=True, stop=False, skip_group_check=True)
                    mm(pv_out[:, h, 0:HD], ph[:, h, :], vl[:, odd, p, h, :], start=False, stop=False, skip_group_check=True)
                    m = mm(pv_out[:, h, :], pl[:, h, :], vh[:, odd, p, h, :], start=False, stop=True, skip_group_check=True)
                m.then_inc(s_pv, 1)

            def transpose_attended(t, k):
                pe.wait_ge(s_av, t + 1)
                need(pe, s_fin, t)
                for c in range(KC):
                    m = nc.tensor.transpose(at_out[:, c, :],
                                            av[:, 4 * c:4 * c + 4, :].rearrange("p h d -> p (h d)"),
                                            perm_out[:, 1 if k % 4 == PAIRS - 1 else 0, :])
                m.then_inc(s_at, 1)

            def project_out(t):
                pe.wait_ge(s_al, t + 1)
                for c in range(KC):
                    for n_, (a, w) in enumerate(((ath, woh), (ath, wol), (atl, woh))):
                        m = mm(ps_post[0:PT, 0:C], a[:, c, :], w[:, c, :], start=c == 0 and n_ == 0,
                               stop=c == KC - 1 and n_ == 2)
                m.then_inc(s_out, 1)

            def back(n, k, lag):
                return (n, k - lag) if k >= lag else (n - 1, k - lag + 8)

            def step(n, first=False, last=False):
                for k in range(8):
                    t = 8 * n + k
                    scores(t, n, k)
                    if not (first and k < 3):
                        transpose_attended(t - 3, k - 3 + 8)
                    if not (last and k >= 4):
                        units(n, k, 0, last)
                    if not (first and k < 2):
                        attend(t - 2, *back(n, k, 2))
                    if not (last and k >= 4):
                        units(n, k, 1, last)
                    if not (first and k < 1):
                        transposed_scores(t - 1, *back(n, k, 1))
                    if not (first and k < 3):
                        project_out(t - 3)
                    if not (last and k >= 4):
                        units(n, k, 2, last)

            pe.wait_ge(s_init, 8)
            pe.wait_ge(s_zero, 1)
            pe.wait_ge(s_bias, 6)
            step(0, first=True)
            with nc.tensor.Fori(1, LAST) as n:
                step(n)
            step(LAST, last=True)
            end = 8 * (LAST + 1)
            transpose_attended(end - 3, 5)
            attend(end - 2, LAST, 6)
            transposed_scores(end - 1, LAST, 7)
            project_out(end - 3)
            transpose_attended(end - 2, 6)
            attend(end - 1, LAST, 7)
            project_out(end - 2)
            transpose_attended(end - 1, 7)
            project_out(end - 1)


def kernel(x, L0_conv_w_qkv, L0_conv_pos_emb, L0_conv_w_out, L0_conv_b_out):
    import concourse.bacc as bacc
    from concourse.bass_utils import run_bass_kernel_spmd

    arrays = {"x": x, "w_qkv": L0_conv_w_qkv, "pos": L0_conv_pos_emb, "w_out": L0_conv_w_out,
              "b_out": L0_conv_b_out, "tables": constants()}
    arrays = {f"in_{k}": np.ascontiguousarray(v) for k, v in arrays.items()}
    nc = bacc.Bacc("TRN2", target_bir_lowering=False, num_devices=1)
    args = [nc.dram_tensor(k, a.shape, mybir.dt.from_np(a.dtype), kind="ExternalInput").ap() for k, a in arrays.items()]
    out = nc.dram_tensor("out", (B, H, W, C), mybir.dt.float32, kind="ExternalOutput").ap()
    build(nc, *args, out)
    r = run_bass_kernel_spmd(nc, [arrays], core_ids=[0])
    return r.results[0]["out"]
```

```python
from contextlib import ExitStack

import numpy as np

import concourse.bass as bass
from concourse import mybir

B, H, W, C = 16, 56, 56, 384
WS, HEADS, HD = 7, 12, 32
DISP = WS // 2
N = WS * WS
NW = W // WS
ROWS = B * (H // WS)
PAIRS = NW // 2
PT = 2 * N
RT = NW * N
HH = HEADS // 2
PAD = 64
KC = C // 128
GROUPS = 32
GC = C // GROUPS
EPS = 1e-5
TALL = WS - DISP
BIG = 1e30

SP_, SLABS, ST = 112, 4, 7
HALVES = 2 * SLABS
LAST = ROWS // 2 - 1

CONSTS = [("ident", 128), ("perm_in", 2 * PT), ("perm_out", 256), ("flip", 128), ("mask_rows", 512),
          ("picks", 128), ("patterns", 128), ("mask", 4 * N), ("eye", N), ("window", 2), ("own_head", HH),
          ("group", KC * GROUPS), ("mean_of", 128), ("ones", 128)]
CONST_AT, _at = {}, 0
for _name, _n in CONSTS:
    CONST_AT[_name] = (_at, _at + _n)
    _at += _n
CONST_COLS = _at
BIAS_ROWS, MASK_ROWS, MAX_ROWS = (0, 64), (49, 50, 51, 125, 126), (52, 113)


def place(kind, r, wc):
    if kind == 0:
        return r * 2 * WS + wc
    return wc * TALL + r if r < TALL else 2 * WS * TALL + wc * DISP + (r - TALL)


def constants():
    t = {n: np.zeros((128, k), np.float32) for n, k in CONSTS}
    t["ident"][:] = np.eye(128)
    pin = t["perm_in"].reshape(128, 2, PT)
    pout = t["perm_out"].reshape(128, 2, 128)
    for kind in range(2):
        for r in range(WS):
            for wc in range(2 * WS):
                w, c = divmod(wc, WS)
                pin[place(kind, r, wc), kind, w * N + r * WS + c] = 1
                pout[w * PAD + r * WS + c, kind, place(kind, r, wc)] = 1
        pads = [w * PAD + i for w in range(2) for i in range(N, PAD)]
        for n, p in enumerate(pads):
            pout[p, kind, PT + n] = 1
    tok = np.arange(N)
    low, right = tok // WS >= TALL, tok % WS >= TALL
    for w in range(2):
        t["flip"][N - 1 - tok, w * PAD + tok] = 1
        t["eye"][w * PAD + tok, tok] = 1
        t["window"][w * PAD:(w + 1) * PAD, w] = 1
    for at in BIAS_ROWS:
        t["picks"][tok, at + N - 1 - tok] = 1
    for row, pattern in zip(MASK_ROWS, (np.ones(N), right, ~right, low, ~low)):
        t["patterns"][:N, row] = BIG * pattern
    t["own_head"][:] = 1
    for at in MAX_ROWS:
        for w in range(2):
            t["own_head"][at + w * HH:at + (w + 1) * HH] = np.eye(HH)
    rows = t["mask_rows"].reshape(128, 4, 2, PAD)
    mask = t["mask"].reshape(2, PAD, 4, N)
    m = MASK_ROWS
    for bottom in range(2):
        for edge in range(2):
            kind = 2 * bottom + edge
            rows[m[0], kind, :, N:] = -1
            for at in MAX_ROWS:
                for w in range(2):
                    rows[at + w * HH:at + (w + 1) * HH, kind, w, :] = -1
            if edge:
                rows[m[1], kind, 1, :N] = -1.0 * ~right
                rows[m[2], kind, 1, :N] = -1.0 * right
                mask[1, :N, kind] -= BIG * (right[:, None] != right[None, :])
            if bottom:
                rows[m[3], kind, :, :N] = -1.0 * ~low
                rows[m[4], kind, :, :N] = -1.0 * low
                mask[:, :N, kind] -= BIG * (low[:, None] != low[None, :])
    ch = np.arange(C).reshape(KC, 128).T
    t["group"][:] = (ch[:, :, None] // GC == np.arange(GROUPS)).reshape(128, -1)
    t["mean_of"][:] = 1.0 / (SP_ * HALVES)
    t["ones"][:] = 1.0
    return np.concatenate([t[n] for n, _ in CONSTS], axis=1)


def need(eng, sem, value):
    if isinstance(value, int) and value <= 0:
        return
    eng.wait_ge(sem, value)


FILL = [([("q", 0)], [("k", 0)], [("q", 1)]),
        ([("k", 1)], [("q", 2), ("x", 0)], [("k", 2), ("x", 1)]),
        ([("v", 0)], [("x", 2)], [("v", 1)]),
        ([("v", 2)], [], [("v", 3)])]
ROW_UNITS = [u for parts in FILL for part in parts for u in part]
STAT_KINDS = ("mean", "var")
FZ_MEAN, FZ_SPREAD, FZ = 6, 8, 21
MEAN_STEPS, ROOT_STEPS = FZ_SPREAD - 2, FZ - FZ_SPREAD - 1
BS_MADE, SC_MADE = 13, 17
BN_AT = [13, 9, 5, 5, 0, 0, 0, 0]


def step_units(k):
    first, second, third = FILL[k % 4]
    return first, second, [("mean", 0)] * (k == 4) + [("var", 0)] * (k == 5) + third


def all_units(ks):
    return [u for k in ks for part in step_units(k) for u in part]


UNITS = len(all_units(range(8)))
PRO_UNITS = 12 + 2 + 2 + 3 + 13


def unit_at(k, kind, i):
    return len(all_units(range(k))) + all_units([k]).index((kind, i))


def x_before(k):
    return [(k - 1, u, c) for u, c in all_units([k - 1]) if u == "x"] if k else []


assert not any(u == "x" for u, _ in all_units([7]))
X_TICK = [next(k for k in range(4) if ("x", c) in all_units([k])) for c in range(KC)]


ROW_FIRST = PRO_UNITS - 13


def v_unit(n, odd, p):
    if isinstance(n, int) and n == 0 and odd == 0:
        return ROW_FIRST + ROW_UNITS.index(("v", p))
    k = (0 if odd else 4) + (2 if p < 2 else 3)
    return PRO_UNITS + UNITS * (n if odd else n - 1) + unit_at(k, "v", p)


def build(nc, x, w_qkv, pos, w_out, b_out, const, y):
    fp32, f16, bf16, i32 = mybir.dt.float32, mybir.dt.float16, mybir.dt.bfloat16, mybir.dt.int32
    ALU, ACT, AX = mybir.AluOpType, mybir.ActivationFunctionType, mybir.AxisListType
    RMAX = bass.bass_isa.ReduceOp.max

    xt = x.rearrange("b h (e s) c -> b (h e) s c", s=SLABS * ST)

    ctx = ExitStack()
    with ctx:
        def sb(name, shape, dt):
            return ctx.enter_context(nc.sbuf_tensor(name, shape, dt))

        def sem(name):
            return ctx.enter_context(nc.semaphore(name))

        cst = sb("cst", [128, CONST_COLS], fp32)

        def const_of(name, rows=128):
            a, b = CONST_AT[name]
            return cst[0:rows, a:b]

        ident = const_of("ident")
        perm_in = const_of("perm_in", PT).rearrange("p (k n) -> p k n", k=2)
        perm_out = const_of("perm_out").rearrange("p (k n) -> p k n", k=2)
        mask_c = const_of("mask").rearrange("p (k n) -> p k n", k=4)
        group = const_of("group").rearrange("p (c g) -> p c g", c=KC)

        wnat = sb("wnat", [128, 9, C], fp32)
        wonat = sb("wonat", [128, 3, C], fp32)
        wh = sb("wh", [128, KC, 3 * C], f16)
        wl = sb("wl", [128, KC, 3 * C], f16)
        woh = sb("woh", [128, KC, C], f16)
        wol = sb("wol", [128, KC, C], f16)
        brow = sb("brow", [1, C], fp32)
        bout = sb("bout", [PT, C], fp32)
        amax = sb("amax", [128, 3], fp32)
        gmax = sb("gmax", [128, 3], fp32)
        p2 = sb("p2", [128, 3], fp32)
        sg = sb("sg", [128, 3], fp32)
        sc = sb("sc", [128, 8], fp32)
        bn = sb("bn", [128, N], fp32)
        bs = sb("bs", [128, N], fp32)
        bd = sb("bd", [128, N], fp32)
        bhi = sb("bhi", [128, N], f16)
        blo = sb("blo", [128, N], f16)
        bt = sb("bt", [128, 4, 128], f16)
        rb = sb("rb", [128, 2, HH, N], bf16)
        eb = sb("eb", [128, N], bf16)
        tq = sb("tq", [128, 2, N], bf16)
        bc = sb("bc", [128, 4, N], fp32)
        sx = sb("sx", [SP_, 2, ST, C], fp32)
        st6 = sb("st6", [SP_, SLABS, GROUPS, 6], fp32)
        red1 = sb("red1", [SP_, GROUPS], fp32)
        red2 = sb("red2", [SP_, GROUPS], fp32)
        red3 = sb("red3", [SP_, GROUPS], fp32)
        red4 = sb("red4", [SP_, GROUPS], fp32)
        dev = sb("dev", [SP_, SLABS, 2, GROUPS], fp32)
        dev2 = sb("dev2", [SP_, SLABS, 2, GROUPS], fp32)
        meanb = sb("meanb", [128, GROUPS], fp32)
        varb = sb("varb", [128, GROUPS], fp32)
        rs0 = sb("rs0", [128, GROUPS], fp32)
        rs1 = sb("rs1", [128, GROUPS], fp32)
        rs2 = sb("rs2", [128, GROUPS], fp32)
        spread = sb("spread", [128, KC, GROUPS], fp32)
        spread2 = sb("spread2", [128, KC, GROUPS], fp32)
        coef = sb("coef", [128, B + 2, 2 * KC], fp32)
        xs = sb("xs", [PT, 2, PAIRS, C], fp32)
        xb = sb("xb", [PT, 8, C], fp32)
        xn = sb("xn", [128, 2, NW, N], fp32)
        xh = sb("xh", [128, 2, KC, NW, PAD], f16)
        xl = sb("xl", [128, 2, KC, NW, PAD], f16)
        qk = sb("qk", [128, 4, KC, RT], f16)
        stack = sb("stack", [96, 2, 4, 2, KC, RT], f16)
        vh = sb("vh", [128, 2, PAIRS, HEADS, HD + 1], f16)
        vl = sb("vl", [128, 2, PAIRS, HEADS, HD], f16)
        lg = sb("lg", [128, 2, HH, N], fp32)
        mx = sb("mx", [128, 2, HEADS], fp32)
        mw = sb("mw", [128, 2, 2, HH], fp32)
        mt = sb("mt", [128, 2, 128], bf16)
        pf = sb("pf", [128, HEADS, N], fp32)
        ph = sb("ph", [128, HEADS, 2 * PAD], f16)
        pl = sb("pl", [128, HEADS, 2 * PAD], f16)
        rv = sb("rv", [128, HEADS], fp32)
        av = sb("av", [128, HEADS, HD], fp32)
        ath = sb("ath", [128, KC, PT], f16)
        atl = sb("atl", [128, KC, PT], f16)

        ps_sa = ctx.enter_context(nc.psum_tensor("ps_sa", [128, 2, 512], fp32))
        ps_st = ctx.enter_context(nc.psum_tensor("ps_st", [128, 2, 512], fp32))
        ps_pv = ctx.enter_context(nc.psum_tensor("ps_pv", [128, 512], fp32))
        ps_post = ctx.enter_context(nc.psum_tensor("ps_post", [128, 512], fp32))
        ps_pj = [ctx.enter_context(nc.psum_tensor(f"ps_pj{i}", [128, 512], fp32)) for i in range(2)]
        rows_out = ps_sa[:, :, HH * N:(HH + 1) * N]
        pv_out = ps_pv[:, 0:HEADS * (HD + 1)].rearrange("p (h d) -> p h d", h=HEADS)
        at_out = ps_post[:, 0:KC * 128].rearrange("p (c n) -> p c n", c=KC)

        s_const = sem("const_loaded")
        s_init = sem("buffers_set")
        s_zero = sem("score_banks_zeroed")
        s_cast = sem("tables_cast")
        s_pre = sem("scalars_made")
        s_gmax = sem("maxima_spread")
        s_bias = sem("bias_tables_made")
        s_slab = [sem("slab_loaded_first"), sem("slab_loaded_second")]
        s_bn = sem("slab_measured")
        s_fz = sem("statistics_step")
        s_reached = sem("sp_waits_met")
        s_load = [sem("row_loaded_even"), sem("row_loaded_odd")]
        s_stack = [sem("stacks_filled_even"), sem("stacks_filled_odd")]
        s_store = [sem(f"pair_stored_{i}") for i in range(8)]
        s_pj = sem("unit_in_psum")
        s_pjr = sem("unit_taken")
        s_hi = sem("high_part_written")
        s_xh = sem("x_high_written")
        s_xl = sem("x_low_written")
        s_xb = sem("residual_made")
        s_sa = sem("scores_in_psum")
        s_lg = sem("logits_made")
        s_mx = sem("maxima_made")
        s_mh = sem("maxima_high")
        s_ml = sem("maxima_low")
        s_mw = sem("maxima_by_window")
        s_tp = sem("shift_rows_in_psum")
        s_tc = sem("shift_rows_taken")
        s_rb = sem("shift_rows_spread")
        s_st = sem("transposed_scores_in_psum")
        s_ph = sem("probabilities_high")
        s_pl = [sem("probabilities_low_first"), sem("probabilities_low_second")]
        s_pv = sem("attended_in_psum")
        s_rv = sem("sums_inverted")
        s_av = sem("attended_normalized")
        s_at = sem("attended_transposed")
        s_ah = sem("attended_high")
        s_al = sem("attended_low")
        s_out = sem("output_in_psum")
        s_fin = sem("output_made")

        K_LOW, K_HIGH, Q_HIGH, Q_LOW = range(4)
        STACK = 12 * 16
        LOADS = (2 * 3 + 4) * 16
        STORES = [32, 32, 32, 64]

        def unit_count(n, k, kind, i):
            return PRO_UNITS + UNITS * n + unit_at(k, kind, i) + 1

        def hi_index(n, k, kind, i):
            before = 10 + 20 * n + 10 * (k // 4)
            return before + [u for u in ROW_UNITS if u[0] != "x"].index((kind, i))

        def x_units(n, k, c):
            return 6 + 6 * n + 3 * (k // 4) + c

        def x_free(n, odd):
            if isinstance(n, int) and n == 0 and not odd:
                return ROW_FIRST + ROW_UNITS.index(("v", PAIRS - 1)) + 1
            return unit_count(n if odd else n - 1, 3 if odd else 7, "v", PAIRS - 1)

        def move_row(eng, dram_, tile_of, sems, pair, load, at):
            na, nb = TALL, DISP
            image, row_a, row_b = at
            dram = dram_[image]
            split = 2 * WS * na
            pieces = []
            if pair < PAIRS - 1:
                c0 = 2 * WS * pair + DISP
                pieces.append((0, split, dram[bass.ds(row_a, na), c0:c0 + 2 * WS, :]))
                pieces.append((split, PT, dram[bass.ds(row_b, nb), c0:c0 + 2 * WS, :]))
            else:
                c0, k = 2 * WS * pair + DISP, 2 * WS - DISP
                pieces.append((0, k * na, dram[bass.ds(row_a, na), c0:W, :].rearrange("r c f -> c r f")))
                pieces.append((k * na, split, dram[bass.ds(row_a, na), 0:DISP, :].rearrange("r c f -> c r f")))
                pieces.append((split, split + k * nb, dram[bass.ds(row_b, nb), c0:W, :].rearrange("r c f -> c r f")))
                pieces.append((split + k * nb, PT, dram[bass.ds(row_b, nb), 0:DISP, :].rearrange("r c f -> c r f")))
            for a, b, d in pieces:
                t = tile_of[a:b]
                if load:
                    eng.dma_start(t, d).then_inc(sems, 16)
                else:
                    eng.dma_start(d, t).then_inc(sems, 16)

        def rows_of(n, odd):
            first = 2 * WS * (n & 3) + WS * odd
            after = 2 * WS * ((n + 1) & 3) if odd else first + WS
            return (n >> 2) & (B - 1), first + DISP, after

        def bias_kind(n, odd, pair):
            edge = 1 if pair == PAIRS - 1 else 0
            if not odd:
                return edge
            return (((n & 3) + 1) >> 2) * 2 + edge

        block = ctx.enter_context(nc.Block())

        @block.sync
        def _(sp):
            sp.dma_start(cst[:, :], const[:, :]).then_inc(s_const, 16)
            sp.dma_start(wnat[:, :, :], w_qkv.rearrange("(a p) c -> p a c", p=128)).then_inc(s_const, 16)
            sp.dma_start(wonat[:, :, :], w_out.rearrange("(a p) c -> p a c", p=128)).then_inc(s_const, 16)
            sp.dma_start(brow[:, :], b_out.rearrange("(a c) -> a c", a=1)).then_inc(s_const, 16)
            def slab(img, s, b):
                sp.dma_start(sx[:, b, :, :], xt[img, :, s * ST:(s + 1) * ST, :]).then_inc(s_slab[b], 16)
            slab(0, 0, 0)
            slab(0, 1, 1)
            sp.wait_ge(s_init, 1)
            row = 2 * WS - 1
            for r in range(WS):
                windows = bass.AP(pos.tensor, r * row, [[1, WS], [row, WS], [1, WS]])
                for at in (0, 64):
                    q = at + r * WS
                    sp.dma_start(bn[q:q + WS, :].rearrange("p (r c) -> p r c", r=WS), windows).then_inc(s_const, 16)
            def load_row(n, odd):
                at = rows_of(n, odd)
                for p in range(PAIRS):
                    move_row(sp, x, xs[:, odd, p, :], s_load[odd], p, True, at)
            load_row(0, 0)
            load_row(0, 1)
            for s in range(2, SLABS):
                sp.wait_ge(s_bn, s - 1)
                slab(0, s, s % 2)
            sp.wait_ge(s_bn, SLABS - 1)
            slab(1, 0, 0)
            sp.wait_ge(s_bn, SLABS + 1)
            slab(1, 1, 0)

            def reach(sem, value):
                if not (isinstance(value, int) and value <= 0):
                    sp.wait_ge(sem, value)
                    sp.sem_inc(s_reached, 1)

            def stack_row(b, done_units, free):
                reach(s_pjr, done_units)
                reach(s_st, free)
                for part, (kp, qp) in enumerate(((K_HIGH, Q_HIGH), (K_HIGH, Q_LOW), (K_LOW, Q_HIGH))):
                    to = slice(32 * part, 32 * part + 32)
                    for g in range(4):
                        sp.dma_start(stack[to, b, g, :, :, :],
                                     qk[32 * g:32 * g + 32, kp:qp + 1:qp - kp, :, :]).then_inc(s_stack[b], 16)

            stack_row(0, ROW_FIRST + ROW_UNITS.index(("k", KC - 1)) + 1, 0)

            def step(n, first=False, last=False):
                for k in range(8):
                    odd, p, t = k // 4, k % 4, 8 * n + k
                    if p == 0 and not last:
                        reach(s_xb, 8 * n + 4 * odd + 4)
                        reach(s_pj, ROW_FIRST + 13 if first and odd else
                             (ROW_FIRST if first else unit_count(n - 1, 4 * odd + X_TICK[2], "x", 2)))
                        load_row(n + 1, odd)
                    if p == 2 and not (last and odd):
                        stack_row(1 - odd, unit_count(n, 4 * odd + 1, "k", 2), 8 * n + 4 * odd)
                    if k == 5 and not last:
                        m = n + 2
                        reach(s_bn, SLABS + 2 + n)
                        slab_at = (m & 3) * ST
                        img = ((m >> 2) + 1) & (B - 1)
                        sp.dma_start(sx[:, 0, :, :], xt[img, :, bass.ds(slab_at, ST), :]).then_inc(s_slab[0], 16)
                    if not (first and k < 3):
                        store(t - 3, n, k - 3)

            def store(t, n, j):
                reach(s_fin, t + 1)
                if j < 0:
                    n, j = n - 1, j + 8
                at = rows_of(n, j // 4)
                move_row(sp, y, xb[:, j, :], s_store[j], j % 4, False, at)

            step(0, first=True)
            with nc.sync.Fori(1, LAST) as n:
                step(n)
            step(LAST, last=True)
            for j in range(5, 8):
                store(8 * LAST + j, LAST, j)
            for j in range(8):
                sp.wait_ge(s_store[j], STORES[j % 4] * (LAST + 1))

        @block.gpsimd
        def _(pool):
            nc.gpsimd.memset(bn[:, :], 0.0).then_inc(s_init, 1)
            nc.gpsimd.memset(xh[:, :, :, :, :], 0.0).then_inc(s_init, 1)
            nc.gpsimd.memset(xl[:, :, :, :, :], 0.0).then_inc(s_init, 1)
            nc.gpsimd.memset(vh[:, :, :, :, :], 1.0).then_inc(s_init, 1)
            nc.gpsimd.memset(ph[:, :, :], 0.0).then_inc(s_init, 1)
            nc.gpsimd.memset(pl[:, :, :], 0.0).then_inc(s_init, 1)
            pool.wait_ge(s_init, 5)
            for w in range(2):
                nc.gpsimd.memset(ph[:, :, w * PAD + N:(w + 1) * PAD], 1.0).then_inc(s_init, 1)
            pool.wait_ge(s_pre, 3)
            nc.gpsimd.partition_all_reduce(gmax[:, :], amax[:, :], 128, RMAX).then_inc(s_gmax, 1)

            def x_low(unit, index, slot, b, c, used):
                pool.wait_ge(s_pjr, unit)
                pool.wait_ge(s_xh, index + 1)
                need(pool, s_pj, used)
                nc.gpsimd.tensor_tensor(xl[:, b, c, :, 0:N], xn[:, slot, :, :], xh[:, b, c, :, 0:N],
                                        ALU.subtract).then_inc(s_xl, 1)

            def residual(n, j):
                if j >= 8:
                    n, j = n + 1, j - 8
                pool.wait_ge(s_load[j // 4], LOADS * (n + 1))
                need(pool, s_store[j], STORES[j % 4] * n)
                nc.gpsimd.tensor_tensor(xb[:, j, :], xs[:, j // 4, j % 4, :], bout[:, :], ALU.add).then_inc(s_xb, 1)

            for c in range(KC):
                x_low(ROW_FIRST - KC + c + 1, c, c % 2, 0, c, 0)
            for c in range(KC):
                x_low(ROW_FIRST + ROW_UNITS.index(("x", c)) + 1, KC + c, (KC + c) % 2, 1, c, 0)
            pool.wait_ge(s_pjr, 14)
            for j in range(3):
                residual(0, j)

            def split_probabilities(t, x_lows):
                pool.wait_ge(s_rb, t + 1)
                pool.wait_ge(s_xb, min(t + 5, 8 * (LAST + 1)) if isinstance(t, int) else t + 5)
                pool.wait_ge(s_xl, x_lows)
                pool.wait_ge(s_ph, t + 1)
                need(pool, s_pv, t)
                nc.gpsimd.tensor_tensor(pl[PAD:, :, PAD:PAD + N], pf[PAD:, :, :], ph[PAD:, :, PAD:PAD + N],
                                        ALU.subtract).then_inc(s_pl[1], 1)

            def x_lows(n, k):
                for at, kind, c in x_before(k):
                    odd = at // 4
                    x_low(unit_count(n, at, kind, c), x_units(n, at, c), (odd + c) % 2, odd, c, x_free(n, odd))

            def step(n, first=False, last=False):
                for k in range(8):
                    t = 8 * n + k
                    if not (last and k >= 4):
                        x_lows(n, k)
                    if not (last and k + 3 >= 8):
                        residual(n, k + 3)
                    if not (first and k < 1):
                        earlier = sum(len(x_before(i)) for i in range(min(k + 1, 4) if last else k + 1))
                        split_probabilities(t - 1, 6 + 6 * n + earlier)
                        pool.wait_ge(s_pl[1], t)
                    pool.wait_ge(s_tc, t + 1)
                    nc.gpsimd.tensor_tensor(
                        rb[:, :, :, :], tq[:, :, :].unsqueeze(2).broadcast_to([128, 2, HH, N]),
                        const_of("own_head").unsqueeze(1).unsqueeze(3).broadcast_to([128, 2, HH, N]),
                        ALU.mult).then_inc(s_rb, 1)

            step(0, first=True)
            with nc.gpsimd.Fori(1, LAST) as n:
                step(n)
            step(LAST, last=True)
            split_probabilities(8 * (LAST + 1) - 1, 6 * LAST + 9)

        @block.scalar
        def _(act):
            def high(unit, kind, i, b, p_free, stack_sem, stack_need, bank):
                act.wait_ge(s_pj, unit)
                if kind == "v":
                    need(act, s_pv, p_free)
                    nc.scalar.activation(vh[:, b, i, :, 0:HD], ps_pj[bank][:, 0:C].rearrange("p (h d) -> p h d", h=HEADS),
                                         ACT.Copy).then_inc(s_hi, 1)
                else:
                    need(act, stack_sem, stack_need)
                    nc.scalar.activation(qk[:, K_HIGH if kind == "k" else Q_HIGH, i, :], ps_pj[bank][:, 0:RT],
                                         ACT.Copy).then_inc(s_hi, 1)

            def x_high(unit, slot, b, c, used):
                act.wait_ge(s_pjr, unit)
                need(act, s_pj, used)
                nc.scalar.activation(xh[:, b, c, :, 0:N], xn[:, slot, :, :], ACT.Copy).then_inc(s_xh, 1)

            act.wait_ge(s_init, 8)
            for c in range(KC):
                x_high(ROW_FIRST - KC + c + 1, c % 2, 0, c, 0)
            u = ROW_FIRST
            for kind, i in ROW_UNITS:
                if kind == "x":
                    x_high(u + 1, (KC + i) % 2, 1, i, 0)
                else:
                    high(u + 1, kind, i, 0, 0, None, 0, u % 2)
                u += 1

            def units(n, k, part):
                base = PRO_UNITS + UNITS * n
                odd = k // 4
                for kind, i in step_units(k)[part]:
                    j = unit_at(k, kind, i)
                    if kind not in STAT_KINDS and kind != "x":
                        high(base + j + 1, kind, i, 1 - odd, 8 * n + 4 * odd - 4 + i + 1,
                             s_stack[odd], STACK * (n + 1), j % 2)

            def x_highs(n, k):
                for at, kind, c in x_before(k):
                    odd = at // 4
                    x_high(unit_count(n, at, kind, c), (odd + c) % 2, odd, c, x_free(n, odd))

            def step(n, first=False, last=False):
                for k in range(8):
                    t = 8 * n + k
                    if not (first and k < 3):
                        attended_high(t - 3)
                    if not (last and k >= 4):
                        units(n, k, 0)
                        x_highs(n, k)
                        units(n, k, 1)
                    if not (first and k < 1):
                        probabilities(t - 1)
                    shift_rows(t)
                    if not (last and k >= 4):
                        units(n, k, 2)

            def attended_high(t):
                act.wait_ge(s_at, t + 1)
                need(act, s_out, t)
                nc.scalar.activation(ath[:, :, :], at_out[:, :, 0:PT], ACT.Copy).then_inc(s_ah, 1)

            def shift_rows(t):
                act.wait_ge(s_tp, t + 1)
                need(act, s_rb, t)
                nc.scalar.activation(tq[:, :, :], rows_out, ACT.Copy).then_inc(s_tc, 1)

            def probabilities(t):
                act.wait_ge(s_st, t + 1)
                for w in range(2):
                    need(act, s_pl[w], t)
                nc.scalar.activation(pf[:, :, :].rearrange("p (a h) n -> p a (h n)", a=2), ps_st[:, :, 0:HH * N], ACT.Exp,
                                     scale=sc[:, 0:1])
                need(act, s_pv, t)
                for w in range(2):
                    rows = slice(w * PAD, (w + 1) * PAD)
                    e = nc.scalar.activation(
                        ph[rows, :, w * PAD:w * PAD + N].rearrange("p (a h) n -> p a h n", a=2),
                        ps_st[rows, :, 0:HH * N].rearrange("p a (h n) -> p a h n", h=HH), ACT.Exp, scale=sc[rows, 0:1])
                e.then_inc(s_ph, 1)

            act.wait_ge(s_pre, SC_MADE)
            step(0, first=True)
            with nc.scalar.Fori(1, LAST) as n:
                step(n)
            step(LAST, last=True)
            end = 8 * (LAST + 1)
            attended_high(end - 3)
            probabilities(end - 1)
            attended_high(end - 2)
            attended_high(end - 1)

        @block.vector
        def _(dve):
            made = [0]

            def pre(ins):
                made[0] += 1
                ins.then_inc(s_pre, 1)
                dve.wait_ge(s_pre, made[0])

            def measure(slab_slot, groups, done, b=0):
                for g in groups:
                    last = nc.vector.bn_stats(st6[:, slab_slot, g, :], sx[:, b, :, g * GC:(g + 1) * GC])
                if done:
                    last.then_inc(s_bn, 1)

            nc.vector.memset(ps_sa[:, :, :], 0.0).then_inc(s_zero, 1)
            dve.wait_ge(s_slab[0], 16)
            measure(0, range(GROUPS), True)
            dve.wait_ge(s_const, 16 * (4 + 2 * WS))
            nc.vector.tensor_reduce(amax[:, 0:1], wnat[:, :, :], AX.XY, ALU.max, apply_absolute_value=True).then_inc(s_pre, 1)
            nc.vector.tensor_reduce(amax[:, 1:2], wonat[:, :, :], AX.XY, ALU.max, apply_absolute_value=True).then_inc(s_pre, 1)
            nc.vector.tensor_reduce(amax[:, 2:3], bn[:, :], AX.X, ALU.max, apply_absolute_value=True).then_inc(s_pre, 1)
            made[0] = 3
            dve.wait_ge(s_gmax, 1)
            pre(nc.vector.tensor_scalar(gmax[:, 0:2], gmax[:, 0:2], 2.0 ** -20, None, ALU.max))
            pre(nc.vector.tensor_scalar(p2[:, 0:2].bitcast(i32), gmax[:, 0:2].bitcast(i32), 0x7F800000, None, ALU.bitwise_and))
            pre(nc.vector.reciprocal(sg[:, 0:2], p2[:, 0:2]))
            pre(nc.vector.scalar_tensor_tensor(sc[:, 0:1], p2[:, 0:1], HD ** -0.5, p2[:, 0:1], ALU.mult, ALU.mult))
            pre(nc.vector.scalar_tensor_tensor(sc[:, 1:2], sg[:, 0:1], HD ** 0.5, sg[:, 0:1], ALU.mult, ALU.mult))
            pre(nc.vector.tensor_tensor(sc[:, 2:3], p2[:, 0:1], p2[:, 1:2], ALU.mult))
            pre(nc.vector.tensor_scalar(gmax[:, 2:3], gmax[:, 2:3], sc[:, 1:2], 2.0 ** -60, ALU.mult, ALU.max))
            pre(nc.vector.tensor_scalar(p2[:, 2:3].bitcast(i32), gmax[:, 2:3].bitcast(i32), 0x7F800000, None, ALU.bitwise_and))
            pre(nc.vector.reciprocal(sg[:, 2:3], p2[:, 2:3]))
            pre(nc.vector.tensor_scalar(bs[:, :], bn[:, :], sc[:, 1:2], None, ALU.mult))
            assert made[0] == BS_MADE
            pre(nc.vector.tensor_scalar(bd[:, :], bs[:, :], sg[:, 2:3], None, ALU.mult))
            pre(nc.vector.tensor_copy(bhi[:, :], bd[:, :]))
            pre(nc.vector.tensor_tensor(blo[:, :], bd[:, :], bhi[:, :], ALU.subtract))
            pre(nc.vector.tensor_copy(bt[:, :, :].rearrange("p a b -> p (a b)"), const_of("mask_rows")))
            for w in range(2):
                cols = slice(w * PAD, w * PAD + N)
                for part, at in ((bhi, 0), (blo, 64)):
                    nc.vector.tensor_copy(bt[at:at + N, :, cols],
                                          part[at:at + N, :].unsqueeze(1).broadcast_to([N, 4, N])).then_inc(s_bias, 1)
            for hh in range(2):
                nc.vector.scalar_tensor_tensor(mt[:, hh, :], const_of("picks"), p2[:, 2:3], const_of("patterns"),
                                               ALU.mult, ALU.add).then_inc(s_bias, 1)
            nc.vector.tensor_copy(eb[:, :], const_of("eye")).then_inc(s_bias, 1)
            dve.wait_ge(s_bias, 7)
            assert made[0] == SC_MADE

            u = 0
            for kind in ("w", "o"):
                for c in range(KC):
                    for a in range(3 if kind == "w" else 1):
                        hi_, lo_ = (wh, wl) if kind == "w" else (woh, wol)
                        s = sg[:, 0:1] if kind == "w" else sg[:, 1:2]
                        cols = slice(a * C, (a + 1) * C)
                        dve.wait_ge(s_pj, u + 1)
                        nc.vector.tensor_scalar(hi_[:, c, cols], ps_pj[u % 2][:, 0:C], s, None, ALU.mult).then_inc(s_cast, 1)
                        dve.wait_ge(s_cast, u + 1)
                        nc.vector.scalar_tensor_tensor(lo_[:, c, cols], ps_pj[u % 2][:, 0:C], s, hi_[:, c, cols],
                                                       ALU.mult, ALU.subtract).then_inc(s_pjr, 1)
                        u += 1
            dve.wait_ge(s_pj, u + 1)
            nc.vector.tensor_tensor(bc[:, :, :], mask_c, ps_pj[u % 2][:, 0:N].unsqueeze(1).broadcast_to([128, 4, N]),
                                    ALU.add).then_inc(s_pjr, 1)
            u += 1
            dve.wait_ge(s_pj, u + 1)
            nc.vector.tensor_copy(bout[:, :], ps_pj[u % 2][0:PT, 0:C]).then_inc(s_pjr, 1)
            u += 1

            def stat_sums():
                nc.vector.tensor_reduce(red1[:, :], st6[:, :, :, 1:5:3].rearrange("p s g e -> p g s e"), AX.XY,
                                        ALU.add).then_inc(s_fz, 1)
                nc.vector.tensor_reduce(red2[:, :], st6[:, :, :, 2:6:3].rearrange("p s g e -> p g s e"), AX.XY,
                                        ALU.add).then_inc(s_fz, 1)

            def stat_mean(unit, bank):
                dve.wait_ge(s_pj, unit)
                nc.vector.tensor_copy(meanb[:, :], ps_pj[bank][:, 0:GROUPS]).then_inc(s_pjr, 1)

            def stat_after_mean(slot, base, i):
                dve.wait_ge(s_fz, base + 2 + i)
                if i == 0:
                    ins = nc.vector.tensor_tensor(dev[:, :, :, :], st6[:, :, :, 1:5:3].rearrange("p s g e -> p s e g"),
                                                  meanb[0:SP_, :].unsqueeze(1).unsqueeze(1).broadcast_to(
                                                      [SP_, SLABS, 2, GROUPS]), ALU.subtract)
                elif i == 1:
                    ins = nc.vector.tensor_tensor(dev2[:, :, :, :], dev[:, :, :, :], dev[:, :, :, :], ALU.mult)
                elif i == 2:
                    ins = nc.vector.tensor_reduce(red3[:, :], dev2[:, :, :, :].rearrange("p s e g -> p g (s e)"), AX.X,
                                                  ALU.add)
                elif i == 3:
                    ins = nc.vector.scalar_tensor_tensor(red4[:, :], red2[:, :], 2.0 / (ST * GC), red3[:, :], ALU.mult,
                                                         ALU.add)
                elif i == 4:
                    ins = nc.vector.tensor_tensor(spread[:, :, :], group, meanb[:, :].unsqueeze(1).broadcast_to(
                        [128, KC, GROUPS]), ALU.mult)
                else:
                    ins = nc.vector.tensor_reduce(coef[:, slot, 0:KC], spread[:, :, :], AX.X, ALU.add)
                ins.then_inc(s_fz, 1)

            def stat_var(unit, bank):
                dve.wait_ge(s_pj, unit)
                nc.vector.tensor_scalar(varb[:, :], ps_pj[bank][:, 0:GROUPS], EPS, None, ALU.add).then_inc(s_pjr, 1)
                dve.wait_ge(s_pjr, unit)
                nc.vector.tensor_scalar(rs1[:, :].bitcast(i32), varb[:, :].bitcast(i32), 1, None,
                                        ALU.logical_shift_right).then_inc(s_fz, 1)

            def stat_root(slot, base, i):
                v, y = varb[:, :], rs0[:, :]
                dve.wait_ge(s_fz, base + FZ_SPREAD + 1 + i)
                if i == 0:
                    ins = nc.vector.tensor_scalar(y.bitcast(i32), rs1[:, :].bitcast(i32), -1.0, float(0x5F3759DF),
                                                  ALU.mult, ALU.add)
                elif i < 10 and i % 3 == 1:
                    ins = nc.vector.scalar_tensor_tensor(rs1[:, :], y, -0.5, v, ALU.mult, ALU.mult)
                elif i < 10 and i % 3 == 2:
                    ins = nc.vector.tensor_tensor(rs2[:, :], rs1[:, :], y, ALU.mult)
                elif i < 10:
                    ins = nc.vector.scalar_tensor_tensor(y, rs2[:, :], 1.5, y, ALU.add, ALU.mult)
                elif i == 10:
                    ins = nc.vector.tensor_tensor(spread2[:, :, :], group, y.unsqueeze(1).broadcast_to(
                        [128, KC, GROUPS]), ALU.mult)
                else:
                    ins = nc.vector.tensor_reduce(coef[:, slot, KC:2 * KC], spread2[:, :, :], AX.X, ALU.add)
                ins.then_inc(s_fz, 1)

            for s in range(1, SLABS):
                dve.wait_ge(s_slab[s % 2], 16 * (s // 2 + 1))
                measure(s, range(GROUPS), True, s % 2)
            dve.wait_ge(s_bn, SLABS)
            stat_sums()
            stat_mean(u + 1, u % 2)
            dve.wait_ge(s_pjr, u + 1)
            for i in range(MEAN_STEPS):
                stat_after_mean(0, 0, i)
            stat_var(u + 2, (u + 1) % 2)
            for i in range(ROOT_STEPS):
                stat_root(0, 0, i)
            u += 2
            dve.wait_ge(s_slab[0], 16 * 3)
            measure(0, range(GROUPS), True)
            dve.wait_ge(s_fz, FZ)

            def x_norm(unit, bank, index, slot, img, c):
                dve.wait_ge(s_pj, unit)
                need(dve, s_xh, index - 1)
                need(dve, s_xl, index - 1)
                nc.vector.tensor_scalar(xn[:, slot, :, :].rearrange("p w n -> p (w n)"), ps_pj[bank][:, 0:RT],
                                        coef[:, img, c:c + 1], coef[:, img, KC + c:KC + c + 1],
                                        ALU.subtract, ALU.mult).then_inc(s_pjr, 1)

            def low(bank, hi, kind, i, b, p_free, stack_sem, stack_need):
                dve.wait_ge(s_hi, hi)
                if kind == "v":
                    need(dve, s_pv, p_free)
                    nc.vector.tensor_tensor(vl[:, b, i, :, :], ps_pj[bank][:, 0:C].rearrange("p (h d) -> p h d", h=HEADS),
                                            vh[:, b, i, :, 0:HD], ALU.subtract).then_inc(s_pjr, 1)
                else:
                    need(dve, stack_sem, stack_need)
                    hp, lp = (K_HIGH, K_LOW) if kind == "k" else (Q_HIGH, Q_LOW)
                    nc.vector.tensor_tensor(qk[:, lp, i, :], ps_pj[bank][:, 0:RT], qk[:, hp, i, :],
                                            ALU.subtract).then_inc(s_pjr, 1)

            for c in range(KC):
                x_norm(u + 1, u % 2, c, c % 2, 0, c)
                u += 1
            h = 0
            for kind, i in ROW_UNITS:
                if kind == "x":
                    x_norm(u + 1, u % 2, KC + i, (KC + i) % 2, 0, i)
                else:
                    low(u % 2, h + 1, kind, i, 0, 0, None, 0)
                    h += 1
                u += 1
            assert u == PRO_UNITS

            def units(n, k, part):
                base, odd = PRO_UNITS + UNITS * n, k // 4
                for kind, i in step_units(k)[part]:
                    j = unit_at(k, kind, i)
                    if kind == "x":
                        if i == 0:
                            dve.wait_ge(s_fz, FZ * (n + 1))
                        x_norm(base + j + 1, j % 2, x_units(n, k, i), (odd + i) % 2, (n + 1) >> 2, i)
                    elif kind == "mean":
                        stat_mean(base + j + 1, j % 2)
                    elif kind == "var":
                        stat_var(base + j + 1, j % 2)
                    else:
                        low(j % 2, hi_index(n, k, kind, i) + 1, kind, i, 1 - odd,
                            8 * n + 4 * odd - 4 + i + 1, s_stack[odd], STACK * (n + 1))

            def logits(t, n, k):
                dve.wait_ge(s_sa, t + 1)
                bias = bc[:, bias_kind(n, k // 4, k % 4), :]
                nc.vector.tensor_tensor(lg[:, :, :, :], ps_sa[:, :, 0:HH * N].rearrange("p a (h n) -> p a h n", h=HH),
                                        bias.unsqueeze(1).unsqueeze(1).broadcast_to([128, 2, HH, N]),
                                        ALU.add).then_inc(s_lg, 1)

            def attended_low(t):
                dve.wait_ge(s_ah, t + 1)
                need(dve, s_out, t)
                nc.vector.tensor_tensor(atl[:, :, :], at_out[:, :, 0:PT], ath[:, :, :], ALU.subtract).then_inc(s_al, 1)

            def maxima(t, k):
                dve.wait_ge(s_lg, t + 1)
                nc.vector.tensor_reduce(mx[:, k % 2, :], lg[:, :, :, :].rearrange("p a h n -> p (a h) n"), AX.X,
                                        ALU.max).then_inc(s_mx, 1)

            def maxima_by_window(t, k):
                dve.wait_ge(s_mx, t + 1)
                nc.vector.tensor_tensor(
                    mw[:, :, :, :], mx[:, k % 2, :].rearrange("p (a h) -> p a h", a=2).unsqueeze(2).broadcast_to([128, 2, 2, HH]),
                    const_of("window").unsqueeze(1).unsqueeze(3).broadcast_to([128, 2, 2, HH]), ALU.mult).then_inc(s_mw, 1)

            def max_columns(part):
                at = MAX_ROWS[part]
                return mt[:, :, at:at + 2 * HH].rearrange("p a (w h) -> p a w h", w=2)

            def maxima_high(t):
                dve.wait_ge(s_mw, t + 1)
                need(dve, s_tp, t)
                nc.vector.tensor_copy(max_columns(0), mw[:, :, :, :]).then_inc(s_mh, 1)

            def maxima_low(t):
                dve.wait_ge(s_mh, t + 1)
                nc.vector.tensor_tensor(max_columns(1), mw[:, :, :, :], max_columns(0), ALU.subtract).then_inc(s_ml, 1)

            def invert(t):
                dve.wait_ge(s_pv, t + 1)
                nc.vector.reciprocal(rv[:, :], pv_out[:, :, HD]).then_inc(s_rv, 1)

            def normalize(t):
                dve.wait_ge(s_rv, t + 1)
                need(dve, s_at, t)
                nc.vector.tensor_tensor(av[:, :, :], pv_out[:, :, 0:HD], rv[:, :].unsqueeze(2).broadcast_to([128, HEADS, HD]),
                                        ALU.mult).then_inc(s_av, 1)

            def output(t, j):
                dve.wait_ge(s_out, t + 1)
                dve.wait_ge(s_xb, t + 1)
                nc.vector.scalar_tensor_tensor(xb[:, j % 8, :], ps_post[0:PT, 0:C], sc[0:PT, 2:3], xb[:, j % 8, :],
                                               ALU.mult, ALU.add).then_inc(s_fin, 1)

            def split_probabilities(t):
                dve.wait_ge(s_ph, t + 1)
                need(dve, s_pv, t)
                nc.vector.tensor_tensor(pl[0:PAD, :, 0:N], pf[0:PAD, :, :], ph[0:PAD, :, 0:N],
                                        ALU.subtract).then_inc(s_pl[0], 1)

            def step(n, first=False, last=False):
                measured = 0
                steps = iter([(stat_after_mean, i) for i in range(MEAN_STEPS)] + [(stat_root, i) for i in range(ROOT_STEPS)])

                def between(since=4):
                    if last or k < since:
                        return
                    f, i = next(steps, (None, 0))
                    if f:
                        if f is stat_after_mean and i == 0:
                            dve.wait_ge(s_pjr, unit_count(n, 4, "mean", 0))
                        f(((n + 1) >> 2) + 1, FZ * (n + 1), i)

                for k in range(8):
                    t = 8 * n + k
                    logits(t, n, k)
                    maxima(t, k)
                    if not (last and k >= 4):
                        units(n, k, 0)
                    if not (first and k < 3):
                        attended_low(t - 3)
                    if not last and k == 4:
                        dve.wait_ge(s_bn, SLABS + 2 + n)
                        stat_sums()
                    maxima_by_window(t, k)
                    between(5)
                    maxima_high(t)
                    between(5)
                    maxima_low(t)
                    if not (first and k < 2):
                        invert(t - 2)
                    if not (first and k < 2):
                        normalize(t - 2)
                    if not (last and k >= 4):
                        units(n, k, 1)
                    if not last and k == 0:
                        dve.wait_ge(s_slab[0], 16 * (4 + n))
                    if not last and BN_AT[k]:
                        measure((n + 1) & 3, range(measured, measured + BN_AT[k]), measured + BN_AT[k] == GROUPS)
                        measured += BN_AT[k]
                    between(5)
                    if not (first and k < 3):
                        output(t - 3, k - 3)
                    between(5)
                    if not (first and k < 1):
                        split_probabilities(t - 1)
                    if not (last and k >= 4):
                        units(n, k, 2)
                    between()
                    between()

            step(0, first=True)
            with nc.vector.Fori(1, LAST) as n:
                step(n)
            step(LAST, last=True)
            end = 8 * (LAST + 1)
            attended_low(end - 3)
            invert(end - 2)
            normalize(end - 2)
            output(end - 3, 5)
            split_probabilities(end - 1)
            attended_low(end - 2)
            invert(end - 1)
            normalize(end - 1)
            output(end - 2, 6)
            attended_low(end - 1)
            output(end - 1, 7)

        @block.tensor
        def _(pe):
            mm = nc.tensor.matmul

            def bank_free(unit):
                need(pe, s_pjr, unit - 2)

            pe.wait_ge(s_const, 16 * (4 + 2 * WS))
            u = 0
            for kind in ("w", "o"):
                for c in range(KC):
                    for a in range(3 if kind == "w" else 1):
                        bank_free(u + 1)
                        for i in range(3):
                            src = wnat[:, 3 * a + i, :] if kind == "w" else wonat[:, i, :]
                            m = nc.tensor.transpose(ps_pj[u % 2][:, i * 128:(i + 1) * 128], src[:, c * 128:(c + 1) * 128], ident)
                        m.then_inc(s_pj, 1)
                        u += 1
            bank_free(u + 1)
            pe.wait_ge(s_pre, BS_MADE)
            mm(ps_pj[u % 2][:, 0:N], const_of("flip", N), bs[0:N, :], start=True, stop=True).then_inc(s_pj, 1)
            u += 1
            bank_free(u + 1)
            mm(ps_pj[u % 2][0:PT, 0:C], const_of("ones", 1)[:, 0:PT], brow[:, :], start=True, stop=True).then_inc(s_pj, 1)
            u += 1

            def stat_unit(kind, unit, bank, fz):
                bank_free(unit)
                pe.wait_ge(s_fz, fz)
                mm(ps_pj[bank][:, 0:GROUPS], const_of("mean_of", SP_), (red1 if kind == "mean" else red4)[:, :],
                   start=True, stop=True).then_inc(s_pj, 1)

            stat_unit("mean", u + 1, u % 2, 2)
            stat_unit("var", u + 2, (u + 1) % 2, FZ_MEAN)
            u += 2

            def x_unit(unit, bank, b, c, loaded):
                bank_free(unit)
                pe.wait_ge(s_load[b], loaded)
                for p in range(PAIRS):
                    m = nc.tensor.transpose(ps_pj[bank][:, p * PT:(p + 1) * PT], xs[:, b, p, c * 128:(c + 1) * 128],
                                            perm_in[:, 1 if p == PAIRS - 1 else 0, :])
                m.then_inc(s_pj, 1)

            def project_unit(unit, bank, kind, i, b, x_ready):
                bank_free(unit)
                pe.wait_ge(s_xh, x_ready)
                pe.wait_ge(s_xl, x_ready)
                for c in range(KC):
                    for n_, (xa, wa) in enumerate(((xh, wh), (xh, wl), (xl, wh))):
                        on = dict(start=c == 0 and n_ == 0, stop=c == KC - 1 and n_ == 2)
                        if kind == "v":
                            m = mm(ps_pj[bank][:, 0:C], xa[:, b, c, 2 * i:2 * i + 2, :].rearrange("p w n -> p (w n)"),
                                   wa[:, c, 2 * C:3 * C], **on)
                        else:
                            o = (C if kind == "k" else 0) + i * 128
                            m = mm(ps_pj[bank][:, 0:RT].rearrange("p (w n) -> p w n", w=NW), wa[:, c, o:o + 128],
                                   xa[:, b, c, :, 0:N], **on)
                m.then_inc(s_pj, 1)

            for c in range(KC):
                x_unit(u + 1, u % 2, 0, c, LOADS)
                u += 1
            for kind, i in ROW_UNITS:
                if kind == "x":
                    x_unit(u + 1, u % 2, 1, i, LOADS)
                else:
                    project_unit(u + 1, u % 2, kind, i, 0, KC)
                u += 1

            def units(n, k, part, last):
                base, odd = PRO_UNITS + UNITS * n, k // 4
                for kind, i in step_units(k)[part]:
                    j = unit_at(k, kind, i)
                    if kind == "x":
                        x_unit(base + j + 1, j % 2, odd, i, LOADS * (n + (1 if last else 2)))
                    elif kind in STAT_KINDS:
                        stat_unit(kind, base + j + 1, j % 2, FZ * (n + 1) + (2 if kind == "mean" else FZ_MEAN))
                    else:
                        project_unit(base + j + 1, j % 2, kind, i, 1 - odd, 6 * n + 6 + 3 * odd)

            def score_blocks(out, b, p, hh, transposed, **flags):
                for hi in range(HH):
                    c, g = divmod(hh * HH + hi, 4)
                    for w in range(2):
                        cols = slice((2 * p + w) * N, (2 * p + w + 1) * N)
                        k_, q_ = stack[0:96, b, g, 0, c, cols], stack[0:96, b, g, 1, c, cols]
                        a, r = (k_, q_) if transposed else (q_, k_)
                        m = mm(out[w * PAD:w * PAD + N, hh, hi * N:(hi + 1) * N], a, r, **flags)
                return m

            def scores(t, n, k):
                odd, p = k // 4, k % 4
                if p == 0:
                    pe.wait_ge(s_stack[odd], STACK * (n + 1))
                need(pe, s_lg, t)
                need(pe, s_tc, t)
                for hh in range(2):
                    m = score_blocks(ps_sa, odd, p, hh, False, start=True, stop=True)
                m.then_inc(s_sa, 1)

            def shift_rows(t):
                pe.wait_ge(s_ml, t + 1)
                need(pe, s_tc, t)
                for hh in range(2):
                    m = mm(rows_out[:, hh, :], mt[:, hh, :], eb[:, :], start=True, stop=True)
                m.then_inc(s_tp, 1)

            def transposed_scores(t, n, k):
                odd, p = k // 4, k % 4
                pe.wait_ge(s_rb, t + 1)
                need(pe, s_ph, t)
                kind = bias_kind(n, odd, p)
                for hh in range(2):
                    out = ps_st[:, hh, 0:HH * N]
                    mm(out, bt[:, kind, :], rb[:, hh, :, :].rearrange("p h n -> p (h n)"),
                       start=True, stop=False, skip_group_check=True)
                    m = score_blocks(ps_st, odd, p, hh, True, start=False, stop=True, skip_group_check=True)
                m.then_inc(s_st, 1)

            def attend(t, n, k):
                odd, p = k // 4, k % 4
                for w in range(2):
                    pe.wait_ge(s_pl[w], t + 1)
                pe.wait_ge(s_pjr, v_unit(n, odd, p) + 1)
                need(pe, s_av, t)
                for h in range(HEADS):
                    out, v = pv_out[:, h, :], vh[:, odd, p, h, :]
                    mm(out, ph[:, h, :], v, start=True, stop=False, skip_group_check=True)
                    mm(out[:, 0:HD], ph[:, h, :], vl[:, odd, p, h, :], start=False, stop=False, skip_group_check=True)
                    m = mm(out, pl[:, h, :], v, start=False, stop=True, skip_group_check=True)
                m.then_inc(s_pv, 1)

            def transpose_attended(t, k):
                pe.wait_ge(s_av, t + 1)
                need(pe, s_fin, t)
                for c in range(KC):
                    m = nc.tensor.transpose(at_out[:, c, :],
                                            av[:, 4 * c:4 * c + 4, :].rearrange("p h d -> p (h d)"),
                                            perm_out[:, 1 if k % 4 == PAIRS - 1 else 0, :])
                m.then_inc(s_at, 1)

            def project_out(t):
                pe.wait_ge(s_al, t + 1)
                for c in range(KC):
                    for n_, (a, w) in enumerate(((ath, woh), (ath, wol), (atl, woh))):
                        m = mm(ps_post[0:PT, 0:C], a[:, c, :], w[:, c, :], start=c == 0 and n_ == 0,
                               stop=c == KC - 1 and n_ == 2)
                m.then_inc(s_out, 1)

            def back(n, k, lag):
                return (n, k - lag) if k >= lag else (n - 1, k - lag + 8)

            def step(n, first=False, last=False):
                for k in range(8):
                    t = 8 * n + k
                    scores(t, n, k)
                    if not (first and k < 3):
                        transpose_attended(t - 3, k - 3 + 8)
                    if not (last and k >= 4):
                        units(n, k, 0, last)
                    if not (first and k < 2):
                        attend(t - 2, *back(n, k, 2))
                    if not (last and k >= 4):
                        units(n, k, 1, last)
                    if not (first and k < 1):
                        transposed_scores(t - 1, *back(n, k, 1))
                    if not (first and k < 3):
                        project_out(t - 3)
                    shift_rows(t)
                    if not (last and k >= 4):
                        units(n, k, 2, last)

            pe.wait_ge(s_init, 8)
            pe.wait_ge(s_zero, 1)
            pe.wait_ge(s_bias, 7)
            step(0, first=True)
            with nc.tensor.Fori(1, LAST) as n:
                step(n)
            step(LAST, last=True)
            end = 8 * (LAST + 1)
            transpose_attended(end - 3, 5)
            attend(end - 2, LAST, 6)
            transposed_scores(end - 1, LAST, 7)
            project_out(end - 3)
            transpose_attended(end - 2, 6)
            attend(end - 1, LAST, 7)
            project_out(end - 2)
            transpose_attended(end - 1, 7)
            project_out(end - 1)


def kernel(x, L0_conv_w_qkv, L0_conv_pos_emb, L0_conv_w_out, L0_conv_b_out):
    import concourse.bacc as bacc
    from concourse.bass_utils import run_bass_kernel_spmd

    arrays = {"x": x, "w_qkv": L0_conv_w_qkv, "pos": L0_conv_pos_emb, "w_out": L0_conv_w_out,
              "b_out": L0_conv_b_out, "tables": constants()}
    arrays = {f"in_{k}": np.ascontiguousarray(v) for k, v in arrays.items()}
    nc = bacc.Bacc("TRN2", target_bir_lowering=False, num_devices=1)
    args = [nc.dram_tensor(k, a.shape, mybir.dt.from_np(a.dtype), kind="ExternalInput").ap() for k, a in arrays.items()]
    out = nc.dram_tensor("out", (B, H, W, C), mybir.dt.float32, kind="ExternalOutput").ap()
    build(nc, *args, out)
    r = run_bass_kernel_spmd(nc, [arrays], core_ids=[0])
    return r.results[0]["out"]
```
